# Optimizing a Trainium2 kernel written in Bass

```python
import numpy as np
import jax
import jax.numpy as jnp

def _softmax(x, axis=-1):
    return jax.nn.softmax(x, axis=axis)

def _gelu(x):
    return jax.nn.gelu(x, approximate=True)

def _silu(x):
    return jax.nn.silu(x)

def _sigmoid(x):
    return jax.nn.sigmoid(x)

def _layernorm(x, axis=-1, eps=1e-05):
    m = jnp.mean(x, axis=axis, keepdims=True)
    v = jnp.var(x, axis=axis, keepdims=True)
    return (x - m) / jnp.sqrt(v + eps)

def _scatter_add(tgt, idx, src, axis=0):
    return tgt.at[idx].add(src)

def _segment_sum(src, seg, n):
    return jax.ops.segment_sum(src, seg, n)
kernel_name = 'mk_xattn_ffn_d1_seqx_r4_da533d'

def setup_inputs(seed: int=0):
    np.random.seed(seed)
    _w = jnp.asarray

    def _rec_inputs():
        import jax
        import jax.numpy as jnp
        _rk = jax.random.key(seed)
        x = -0.0003929 + 0.9999 * jax.random.normal(jax.random.fold_in(_rk, 1), (16, 256, 512), jnp.float32)
        _lenS = 256 - jax.random.randint(jax.random.fold_in(_rk, 7), (16,), 0, max(1, 256 // 4) + 1, jnp.int32)
        _lenS2 = 256 - jax.random.randint(jax.random.fold_in(_rk, 8), (16,), 0, max(1, 256 // 4) + 1, jnp.int32)
        _ctx_1024P = jax.random.normal(jax.random.fold_in(_rk, 11), (16, 16, 256), jnp.float32)
        _ctx_1024c = jax.random.dirichlet(jax.random.fold_in(_rk, 511), 0.3 * jnp.ones((16,), jnp.float32), (16, 256))
        _ctx_1024t = jnp.einsum('bsk,bkd->bsd', _ctx_1024c, _ctx_1024P)
        _ctx_1024t = _ctx_1024t * jax.lax.rsqrt(jnp.mean(jnp.square(_ctx_1024t)) + 1e-12) * 0.953939
        ctx_1024 = -0.000494167 + 1.00018 * (_ctx_1024t + 0.3 * jax.random.normal(jax.random.fold_in(_rk, 611), (16, 256, 256), jnp.float32))
        _validS = jnp.arange(256)[None, :] < _lenS[:, None]
        _validS2 = jnp.arange(256)[None, :] < _lenS2[:, None]
        _causal = jnp.tril(jnp.ones((256, 256), dtype=bool))
        mask_BxS2_bf1 = jnp.ones((16, 256), dtype=bool)
        return (x, ctx_1024, mask_BxS2_bf1)
    x, ctx_1024, mask_BxS2_bf1 = _rec_inputs()

    def _L0_xattn_setup():
        import jax, jax.numpy as jnp
        import numpy as np
        N_HEADS = 16
        N_KV_HEADS = 8
        HEAD_DIM = 128
        D_TEXT = 512
        D_VISION = 256
        GROUPS = N_HEADS // N_KV_HEADS
        key = jax.random.key(seed)
        ks = jax.random.split(key, 6)
        B, T_text, T_vis = (4, 512, 144)
        text_hidden = jax.random.normal(ks[0], (B, T_text, D_TEXT), dtype=jnp.float32)
        vision_tokens = jax.random.normal(ks[1], (B, T_vis, D_VISION), dtype=jnp.float32)
        vision_mask = jnp.ones((B, T_vis), dtype=bool)
        s = 0.02
        Wq = jax.random.normal(ks[2], (D_TEXT, N_HEADS * HEAD_DIM), dtype=jnp.float32) * s
        Wk = jax.random.normal(ks[3], (D_VISION, N_KV_HEADS * HEAD_DIM), dtype=jnp.float32) * s
        Wv = jax.random.normal(ks[4], (D_VISION, N_KV_HEADS * HEAD_DIM), dtype=jnp.float32) * s
        Wo = jax.random.normal(ks[5], (N_HEADS * HEAD_DIM, D_TEXT), dtype=jnp.float32) * s
        return {'text_hidden': text_hidden, 'vision_tokens': vision_tokens, 'vision_mask': vision_mask, 'Wq': Wq, 'Wk': Wk, 'Wv': Wv, 'Wo': Wo}
    _L0_xattn_all = _L0_xattn_setup()
    _L0_xattn_in = {k: v for k, v in _L0_xattn_all.items() if k in ('Wq', 'Wk', 'Wv', 'Wo')}
    del _L0_xattn_all

    def _L0_ffn_setup():
        import jax, jax.numpy as jnp
        import numpy as np
        E = 32
        K = 4
        G = 4
        TG = 2
        H = 512
        F = 256
        FS = 512
        SCALE = 2.0
        B, S = (2, 256)
        N = B * S
        CAP = 2 * (N * K // E)

        def _gate(x, gate_w, gate_bias):
            logits = x @ gate_w.T
            scores = jax.nn.sigmoid(logits)
            sc = scores + gate_bias
            n = x.shape[0]
            grp = sc.reshape(n, G, E // G)
            group_scores = jax.lax.top_k(grp, 2)[0].sum(-1)
            _, gidx = jax.lax.top_k(group_scores, TG)
            gmask = jnp.zeros((n, G), sc.dtype).at[jnp.arange(n)[:, None], gidx].set(1.0)
            smask = jnp.repeat(gmask, E // G, axis=1)
            tmp = jnp.where(smask > 0, sc, 0.0)
            _, topk_idx = jax.lax.top_k(tmp, K)
            topk_w = jnp.take_along_axis(scores, topk_idx, axis=1)
            topk_w = topk_w / (topk_w.sum(-1, keepdims=True) + 1e-20)
            return (topk_idx, topk_w * SCALE)

        def _moe(x, topk_idx, topk_w, w1, w2, w3):
            n = x.shape[0]
            flat_e = topk_idx.reshape(-1)
            oh = jax.nn.one_hot(flat_e, E, dtype=jnp.int32)
            pos = (jnp.cumsum(oh, axis=0) * oh).sum(-1) - 1
            keep = pos < CAP
            slot = jnp.where(keep, pos, CAP)
            x_rep = jnp.repeat(x, K, axis=0)
            buf = jnp.zeros((E, CAP, H), x.dtype).at[flat_e, slot].set(x_rep, mode='drop')
            h = jax.nn.silu(jnp.einsum('ech,ehf->ecf', buf, w1)) * jnp.einsum('ech,ehf->ecf', buf, w3)
            ob = jnp.einsum('ecf,efh->ech', h, w2)
            y = ob[flat_e, jnp.minimum(slot, CAP - 1)]
            y = jnp.where(keep[:, None], y, 0.0)
            return (y.reshape(n, K, H) * topk_w[:, :, None]).sum(1)
        key = jax.random.key(seed)
        ks = jax.random.split(key, 9)
        w = 0.02
        return {'hidden_states': jax.random.normal(ks[0], (B, S, H), jnp.float32), 'gate_w': jax.random.normal(ks[1], (E, H), jnp.float32) * w, 'gate_bias': jax.random.normal(ks[2], (E,), jnp.float32) * w, 'w1': jax.random.normal(ks[3], (E, H, F), jnp.float32) * w, 'w2': jax.random.normal(ks[4], (E, F, H), jnp.float32) * w, 'w3': jax.random.normal(ks[5], (E, H, F), jnp.float32) * w, 'shared_gate': jax.random.normal(ks[6], (H, FS), jnp.float32) * w, 'shared_up': jax.random.normal(ks[7], (H, FS), jnp.float32) * w, 'shared_down': jax.random.normal(ks[8], (FS, H), jnp.float32) * w}
    _L0_ffn_all = _L0_ffn_setup()
    _L0_ffn_in = {k: v for k, v in _L0_ffn_all.items() if k in ('gate_w', 'gate_bias', 'w1', 'w2', 'w3', 'shared_gate', 'shared_up', 'shared_down')}
    del _L0_ffn_all
    return {'x': x, 'ctx_1024': ctx_1024, 'mask_BxS2_bf1': mask_BxS2_bf1, 'L0_xattn_Wq': _L0_xattn_in['Wq'], 'L0_xattn_Wk': _L0_xattn_in['Wk'], 'L0_xattn_Wv': _L0_xattn_in['Wv'], 'L0_xattn_Wo': _L0_xattn_in['Wo'], 'L0_ffn_gate_w': _L0_ffn_in['gate_w'], 'L0_ffn_gate_bias': _L0_ffn_in['gate_bias'], 'L0_ffn_w1': _L0_ffn_in['w1'], 'L0_ffn_w2': _L0_ffn_in['w2'], 'L0_ffn_w3': _L0_ffn_in['w3'], 'L0_ffn_shared_gate': _L0_ffn_in['shared_gate'], 'L0_ffn_shared_up': _L0_ffn_in['shared_up'], 'L0_ffn_shared_down': _L0_ffn_in['shared_down']}

def reference(x, ctx_1024, mask_BxS2_bf1, L0_xattn_Wq, L0_xattn_Wk, L0_xattn_Wv, L0_xattn_Wo, L0_ffn_gate_w, L0_ffn_gate_bias, L0_ffn_w1, L0_ffn_w2, L0_ffn_w3, L0_ffn_shared_gate, L0_ffn_shared_up, L0_ffn_shared_down):
    import jax
    import jax.numpy as jnp

    def _L0_xattn_ref(text_hidden, vision_tokens, vision_mask, Wq, Wk, Wv, Wo):
        import jax, jax.numpy as jnp
        import numpy as np
        N_HEADS = 16
        N_KV_HEADS = 8
        HEAD_DIM = 128
        D_TEXT = 512
        D_VISION = 256
        GROUPS = N_HEADS // N_KV_HEADS
        B, T_text, _ = text_hidden.shape
        T_vis = vision_tokens.shape[1]
        scale = jnp.float32(np.sqrt(HEAD_DIM))
        q = (text_hidden @ Wq).reshape(B, T_text, N_HEADS, HEAD_DIM).transpose(0, 2, 1, 3)
        k = (vision_tokens @ Wk).reshape(B, T_vis, N_KV_HEADS, HEAD_DIM).transpose(0, 2, 1, 3)
        v = (vision_tokens @ Wv).reshape(B, T_vis, N_KV_HEADS, HEAD_DIM).transpose(0, 2, 1, 3)
        k = jnp.repeat(k, GROUPS, axis=1)
        v = jnp.repeat(v, GROUPS, axis=1)
        scores = jnp.einsum('bhtd,bhsd->bhts', q, k) / scale
        mask = vision_mask[:, None, None, :]
        scores = jnp.where(mask, scores, -jnp.inf)
        attn = jax.nn.softmax(scores, axis=-1)
        attn = jnp.nan_to_num(attn, nan=0.0)
        out = jnp.einsum('bhts,bhsd->bhtd', attn, v)
        out = out.transpose(0, 2, 1, 3).reshape(B, T_text, N_HEADS * HEAD_DIM)
        return out @ Wo

    def _L0_ffn_ref(hidden_states, gate_w, gate_bias, w1, w2, w3, shared_gate, shared_up, shared_down):
        import jax, jax.numpy as jnp
        import numpy as np
        E = 32
        K = 4
        G = 4
        TG = 2
        H = 512
        F = 256
        FS = 512
        SCALE = 2.0
        B, S = (2, 256)
        N = B * S
        CAP = 2 * (N * K // E)

        def _gate(x, gate_w, gate_bias):
            logits = x @ gate_w.T
            scores = jax.nn.sigmoid(logits)
            sc = scores + gate_bias
            n = x.shape[0]
            grp = sc.reshape(n, G, E // G)
            group_scores = jax.lax.top_k(grp, 2)[0].sum(-1)
            _, gidx = jax.lax.top_k(group_scores, TG)
            gmask = jnp.zeros((n, G), sc.dtype).at[jnp.arange(n)[:, None], gidx].set(1.0)
            smask = jnp.repeat(gmask, E // G, axis=1)
            tmp = jnp.where(smask > 0, sc, 0.0)
            _, topk_idx = jax.lax.top_k(tmp, K)
            topk_w = jnp.take_along_axis(scores, topk_idx, axis=1)
            topk_w = topk_w / (topk_w.sum(-1, keepdims=True) + 1e-20)
            return (topk_idx, topk_w * SCALE)

        def _moe(x, topk_idx, topk_w, w1, w2, w3):
            n = x.shape[0]
            flat_e = topk_idx.reshape(-1)
            oh = jax.nn.one_hot(flat_e, E, dtype=jnp.int32)
            pos = (jnp.cumsum(oh, axis=0) * oh).sum(-1) - 1
            keep = pos < CAP
            slot = jnp.where(keep, pos, CAP)
            x_rep = jnp.repeat(x, K, axis=0)
            buf = jnp.zeros((E, CAP, H), x.dtype).at[flat_e, slot].set(x_rep, mode='drop')
            h = jax.nn.silu(jnp.einsum('ech,ehf->ecf', buf, w1)) * jnp.einsum('ech,ehf->ecf', buf, w3)
            ob = jnp.einsum('ecf,efh->ech', h, w2)
            y = ob[flat_e, jnp.minimum(slot, CAP - 1)]
            y = jnp.where(keep[:, None], y, 0.0)
            return (y.reshape(n, K, H) * topk_w[:, :, None]).sum(1)
        b, s, h = hidden_states.shape
        x = hidden_states.reshape(-1, h)
        topk_idx, topk_w = _gate(x, gate_w, gate_bias)
        out = _moe(x, topk_idx, topk_w, w1, w2, w3)
        shared = jax.nn.silu(x @ shared_gate) * (x @ shared_up) @ shared_down
        return (out + shared).reshape(b, s, h)
    x = x + _L0_xattn_ref(_layernorm(x, axis=-1), ctx_1024, mask_BxS2_bf1, L0_xattn_Wq, L0_xattn_Wk, L0_xattn_Wv, L0_xattn_Wo)
    x = x + _L0_ffn_ref(_layernorm(x, axis=-1), L0_ffn_gate_w, L0_ffn_gate_bias, L0_ffn_w1, L0_ffn_w2, L0_ffn_w3, L0_ffn_shared_gate, L0_ffn_shared_up, L0_ffn_shared_down)
    return x

_drawn_inputs = setup_inputs


def setup_inputs(seed=0):
    import zlib

    import numpy as np

    out = dict(_drawn_inputs(seed))
    spreads = {}
    factors = {'L0_xattn_Wq': 7.164,
     'L0_xattn_Wk': 7.141,
     'L0_ffn_gate_w': 3.461,
     'L0_ffn_gate_bias': 5.787,
     'L0_ffn_w1': 3.322,
     'L0_ffn_w2': 3.253,
     'L0_ffn_w3': 3.257}
    for name, (base, spread) in spreads.items():
        noise = np.random.default_rng([zlib.crc32(name.encode()), seed]).standard_normal(out[name].shape)
        drawn = base * np.exp(spread * noise) if base else spread * noise
        out[name] = jnp.asarray(drawn.astype(out[name].dtype))
    for name, factor in factors.items():
        out[name] = (out[name] * factor).astype(out[name].dtype)
    return out
```

```python
from contextlib import ExitStack

import numpy as np

import concourse.bass as bass
import concourse.mybir as mybir

F32, F16, U32, U8 = mybir.dt.float32, mybir.dt.float16, mybir.dt.uint32, mybir.dt.uint8
ALU = mybir.AluOpType
ACT = mybir.ActivationFunctionType
AX = mybir.AxisListType

P = 128
B, T, D = 16, 256, 512
S, DC = 256, 256
HEADS, KV, HD = 16, 8, 128
PAIR = HEADS // KV
E, TOPK, GROUPS, TOPG = 32, 4, 4, 2
F, FS = 256, 512
ROUTE_SCALE = 2.0
CAP = 2 * (2 * 256 * TOPK // E)
N = B * T
EPG = E // GROUPS

TB, SB, KD, KC, FB, FSB = T // P, S // P, D // P, DC // P, F // P, FS // P
TURNS = B * KV
assert CAP == P

W_S = 64.0
X_S = 64.0
C_S = 16.0
V_S = 16.0
P_S = 1024.0
HS_S = 64.0
HE_S = 16.0
MASKED = 1e30
LN_EPS = 1e-5
SCORE_SCALE = 1.0 / float(np.sqrt(np.float32(HD)))


class Signal:

    def __init__(self, handle):
        self.handle, self.value = handle, 0


class Queue:

    def __init__(self):
        self.steps, self.seen = [], {}

    def wait(self, *marks):
        for mark in marks:
            if mark is None:
                continue
            signal, value = mark
            if self.seen.get(id(signal), 0) < value:
                self.seen[id(signal)] = value
                self.steps.append(lambda eng, h=signal.handle, v=value: eng.wait_ge(h, v))

    def do(self, build, signal=None, by=1):
        if signal is None:
            self.steps.append(build)
            return None
        self.steps.append(lambda eng, h=signal.handle: build(eng).then_inc(h, by))
        signal.value += by
        return (signal, signal.value)

    def run(self, eng):
        for step in self.steps:
            step(eng)


class Split:

    def __init__(self, hi, lo):
        self.hi, self.lo = hi, lo

    def __getitem__(self, at):
        return Split(self.hi[at], self.lo[at])


def build(nc, x, ctx_t, mask, mask_cols, wq, wk, wv, wo, gate_t, gate_bias, w1, w2, w3,
          shared_gate, shared_up, shared_down, out):
    stack = ExitStack()
    with stack:
        def sbuf(name, shape, dt=F32):
            return stack.enter_context(nc.sbuf_tensor(name, [P] + list(shape), dt))

        def split(name, shape):
            both = sbuf(name, [2] + list(shape), F16)
            if len(shape) == 1:
                return Split(both[:, 0, :], both[:, 1, :])
            return Split(both[:, 0], both[:, 1])

        def signal(name):
            return Signal(stack.enter_context(nc.semaphore(name)))

        xn2_rows = nc.dram_tensor("xn2_rows", (N + CAP, D), F32, kind="Internal").ap()
        slot_table = nc.dram_tensor("slot_table", (CAP * E, 2), U32, kind="Internal").ap()

        sizes = [(KC, KV * HD), (KC, KV * HD), (KD, HEADS * HD), (HEADS, D)]
        attention_w = sbuf("attention_w", [sum(2 * k * n for k, n in sizes)], F16)

        def carve():
            at = 0
            for k, n in sizes:
                yield Split(*(attention_w[:, at + i * k * n:at + (i + 1) * k * n].rearrange("p (k n) -> p k n", k=k)
                              for i in (0, 1)))
                at += 2 * k * n
        wv_s, wk_s, wq_s, wo_s = carve()
        sg_s = split("sg_s", [KD, FS])
        su_s = split("su_s", [KD, FS])
        sd_s = split("sd_s", [FSB, D])
        gate_s = split("gate_s", [KD, E])
        CHUNK = 2048
        weight_in = [sbuf(f"weight_in{n}", [CHUNK]) for n in range(2)]

        x_in = [sbuf(f"x_in{n}", [TB, D]) for n in range(2)]
        normed = sbuf("normed", [TB, D])
        xn_t = [split(f"xn_t{n}", [KD, T]) for n in range(2)]
        ctx_in = sbuf("ctx_in", [KC, S])
        ctx_s = [split(f"ctx_s{n}", [KC, S]) for n in range(2)]
        mask_in = sbuf("mask_in", [S], U8)
        mask_add = [sbuf(f"mask_add{n}", [S]) for n in range(2)]
        mask_cols_in = sbuf("mask_cols_in", [B * SB], U8)
        value_scale = sbuf("value_scale", [B * SB])
        v_s = [split(f"v_s{n}", [SB, KV * HD]) for n in range(2)]
        q_t = split("q_t", [PAIR * T])
        k_t = split("k_t", [S])
        probs = sbuf("probs", [PAIR * TB, S])
        neg_max = sbuf("neg_max", [PAIR * TB])
        prob_sum = sbuf("prob_sum", [PAIR * TB])
        prob_inv = sbuf("prob_inv", [PAIR * TB])
        p_t = split("p_t", [SB, PAIR * T])
        o_t = split("o_t", [PAIR * T])
        stats = sbuf("stats", [TB, 6])
        mean_var = sbuf("mean_var", [TB, 2])
        var_eps = sbuf("var_eps", [TB])
        rstd = sbuf("rstd", [TB])
        minus_half = sbuf("minus_half", [TB])
        x1 = sbuf("x1", [TB, D])
        xn2 = sbuf("xn2", [TB, D])
        xn2_t = split("xn2_t", [KD, T])
        tanh_g = sbuf("tanh_g", [T])
        gated = sbuf("gated", [T])
        hidden = sbuf("hidden", [T])
        h_t = split("h_t", [FSB, T])
        bias_row = sbuf("bias_row", [E])
        exp_neg = sbuf("exp_neg", [TB, E])
        score = sbuf("score", [TB, E])
        biased = sbuf("biased", [TB, E])
        group_top = sbuf("group_top", [TB * GROUPS, 8])
        group_score = sbuf("group_score", [TB, GROUPS])
        beats = sbuf("beats", [TB, GROUPS, GROUPS])
        ties = sbuf("ties", [TB, GROUPS, GROUPS])
        lower = sbuf("lower", [GROUPS, GROUPS])
        group_rank = sbuf("group_rank", [TB, GROUPS])
        top8 = sbuf("top8", [TB, 8])
        top8_at = sbuf("top8_at", [TB, 8], U32)
        chosen = sbuf("chosen", [TB, TOPK])
        expert_no = sbuf("expert_no", [E])
        one_hot = sbuf("one_hot", [TB, TOPK, E])
        picked = sbuf("picked", [TB, TOPK, E])
        weight = sbuf("weight", [TB, TOPK])
        weight_sum = sbuf("weight_sum", [TB])
        weight_inv = sbuf("weight_inv", [TB])
        uses = sbuf("uses", [TB, E], F16)
        earlier = sbuf("earlier", [P], F16)
        ones = sbuf("ones", [P], F16)
        taken = sbuf("taken", [E])
        position = sbuf("position", [TB, E])
        my_position = sbuf("my_position", [TB, TOPK])
        slot_f = sbuf("slot_f", [TB, TOPK])
        slot_at = [sbuf(f"slot_at{n}", [TB, TOPK], U32) for n in range(2)]
        entry = [sbuf(f"entry{n}", [TB, TOPK, 2], U32) for n in range(2)]
        ident = sbuf("ident", [P])
        blank = sbuf("blank", [E, 2], U32)

        EW = KD * 2 * F + FB * D
        AHEAD = 3
        expert_in = [attention_w[:, 2 * n * EW:2 * (n + 1) * EW].bitcast(F32) for n in range(AHEAD)]
        expert_w = [Split(attention_w[:, 2 * n * EW:(2 * n + 1) * EW], attention_w[:, (2 * n + 1) * EW:(2 * n + 2) * EW])
                    for n in range(AHEAD, 2 * AHEAD)]
        rows_in = [x_in[0][:, 0, :], x_in[0][:, 1, :], x_in[1][:, 0, :]]
        rows_t = xn_t
        table = sbuf("table", [E, 2], U32)
        slot_weight = sbuf("slot_weight", [E])
        expert_h = normed[:, 0, 0:F]
        expert_h_t = [h_t[:, 0:FB, 0:P], h_t[:, FB:2 * FB, 0:P]]
        expert_y = [weight_in[n // 2][:, (n % 2) * D:(n % 2 + 1) * D] for n in range(4)]

        def bank(name):
            return stack.enter_context(nc.psum_tensor(name, [P, 512], F32))

        ps_score = [bank("ps_score0"), bank("ps_score1")]
        ps_fill = [bank("ps_fill0"), bank("ps_fill1")]
        ps_head = bank("ps_head")
        ps_query = bank("ps_query")
        ps_out = [bank("ps_out0"), bank("ps_out1")]
        bank_free = {}

        sync, pool, act, dve, pe = (Queue() for _ in range(5))

        consts = signal("consts")
        pe_query, pe_key, pe_score, pe_trans = (signal(n) for n in ("pe_query", "pe_key", "pe_score", "pe_trans"))
        pe_head, pe_out, pe_fill = signal("pe_head"), signal("pe_out"), signal("pe_fill")
        act_hi, dve_lo = signal("act_hi"), signal("dve_lo")
        pool_hi = signal("pool_hi")
        dve_max, act_exp, dve_inv, pool_norm = (signal(n) for n in ("dve_max", "act_exp", "dve_inv", "pool_norm"))
        dve_stats, pool_rstd, dve_normed = signal("dve_stats"), signal("pool_rstd"), signal("dve_normed")
        dve_residual, act_fn, dve_glu = signal("dve_residual"), signal("act_fn"), signal("dve_glu")
        dve_route, pool_entry, pool_mask = signal("dve_route"), signal("pool_entry"), signal("pool_mask")
        act_y = signal("act_y")
        in_weight = [signal(f"in_weight{n}") for n in range(2)]
        in_x = [signal(f"in_x{n}") for n in range(2)]
        in_ctx, in_mask, in_const = signal("in_ctx"), signal("in_mask"), signal("in_const")
        out_rows, out_xn2 = signal("out_rows"), signal("out_xn2")
        in_table = signal("in_table")
        scattered = [signal(f"scattered{n}") for n in range(2)]
        gathered = [signal(f"gathered{n}") for n in range(3)]
        in_expert = [signal(f"in_expert{n}") for n in range(AHEAD)]
        added = signal("added")
        out_blank = signal("out_blank")

        mark = {}

        def load(signal_, dst, src, *after):
            sync.wait(*after)
            return sync.do(lambda e: e.dma_start(dst, src), signal_, 16)

        def product(dst, a, b, first, last):
            pe.do(lambda e: e.matmul(dst, a.hi, b.hi, start=first, stop=False))
            pe.do(lambda e: e.matmul(dst, a.hi, b.lo, start=False, stop=False))
            final = lambda e: e.matmul(dst, a.lo, b.hi, start=False, stop=last)
            return final

        def products(dst, pairs, sig=None, first=True, last=True):
            for n, (a, b) in enumerate(pairs):
                final = product(dst, a, b, first and n == 0, last and n == len(pairs) - 1)
                end = n == len(pairs) - 1
                m = pe.do(final, sig if end else None)
            return m

        def split_psum(src, dst, scale, ready, vector_scale=None):
            s = scale if vector_scale is None else vector_scale
            act.wait(ready)
            hi = act.do(lambda e: e.activation(dst.hi, src, ACT.Copy, scale=s), act_hi)
            dve.wait(hi)
            return dve.do(lambda e: e.scalar_tensor_tensor(dst.lo, src, s, dst.hi, ALU.mult, ALU.subtract), dve_lo)

        def split_sbuf(src, dst, scale, ready, free=None):
            pool.wait(ready, free)
            hi = pool.do(lambda e: e.tensor_scalar(dst.hi, src, scale, 1.0, ALU.mult, ALU.mult), pool_hi)
            dve.wait(ready, free, hi)
            return dve.do(lambda e: e.scalar_tensor_tensor(dst.lo, src, scale, dst.hi, ALU.mult, ALU.subtract), dve_lo)

        def constants():
            pool.do(lambda e: e.memset(ident[:, :], 0.0), consts)
            pool.do(lambda e: e.memset(earlier[:, :], 1.0), consts)
            pool.do(lambda e: e.memset(lower[:, :, :], 1.0), consts)
            pool.do(lambda e: e.memset(xn2[:, 0, :], 0.0), consts)
            pool.do(lambda e: e.memset(blank[:, :, 1], 0), consts)
            m = pool.do(lambda e: e.memset(minus_half[:, :], -0.5), consts)
            pool.wait(m)
            pool.do(lambda e: e.affine_select(out=ident[:, :], in_=ident[:, :], compare_op=ALU.not_equal, fill=1.0,
                                              base=0, pattern=[[-1, P]], channel_multiplier=1), consts)
            pool.do(lambda e: e.affine_select(out=earlier[:, :], in_=earlier[:, :], compare_op=ALU.is_gt, fill=0.0,
                                              base=0, pattern=[[1, P]], channel_multiplier=-1), consts)
            pool.do(lambda e: e.affine_select(out=lower[:, :, :], in_=lower[:, :, :], compare_op=ALU.is_gt, fill=0.0,
                                              base=0, pattern=[[1, GROUPS], [-1, GROUPS]], channel_multiplier=0), consts)
            pool.do(lambda e: e.memset(ones[:, :], 1.0), consts)
            pool.do(lambda e: e.memset(taken[:, :], 0.0), consts)
            pool.do(lambda e: e.iota(expert_no[:, :], pattern=[[1, E]], base=0, channel_multiplier=0,
                                     allow_small_or_imprecise_dtypes=True), consts)
            m = pool.do(lambda e: e.iota(blank[:, :, 0], pattern=[[0, E]], base=N, channel_multiplier=1), consts)
            mark["consts"] = m
            for q in (pool, dve, pe, act):
                q.wait(m)
            mark["mask_cols"] = load(in_const, mask_cols_in[:, :], mask_cols)
            load(in_const, bias_row[:, :], gate_bias.broadcast_to([P, E]))
            m = (in_const, in_const.value)
            dve.wait(m)
            mark["value_scale"] = dve.do(lambda e: e.tensor_scalar(value_scale[:, :], mask_cols_in[:, :],
                                                                   V_S / (W_S * C_S), None, ALU.mult), dve_route)
            act.wait(mark["value_scale"])
            dve.wait(mark["value_scale"])

        def blank_rows():
            load(out_blank, slot_table.rearrange("(p e) c -> p (e c)", e=E), blank[:, :, :].rearrange("p e c -> p (e c)"),
                 mark["consts"])
            load(out_blank, xn2_rows[N:N + CAP, :], xn2[:, 0, :])
            load(out_blank, out[N:N + CAP, :], xn2[:, 0, :])
            mark["blank"] = (out_blank, out_blank.value)

        weight_jobs = []

        def weight_job(name, dst, src, rows, cols):
            weight_jobs.append((name, dst, src, rows, cols))

        def rows_of(w):
            return w.rearrange("(k p) n -> p k n", p=P)

        def plan_weights():
            weight_job("wk", wk_s, rows_of(wk), KC, KV * HD)
            weight_job(("wq", 0), wq_s[:, :, 0:512], rows_of(wq)[:, :, 0:512], KD, 512)
            weight_job("wv", wv_s, rows_of(wv), KC, KV * HD)
            for c in range(4):
                if c:
                    weight_job(("wq", c), wq_s[:, :, c * 512:(c + 1) * 512], rows_of(wq)[:, :, c * 512:(c + 1) * 512], KD, 512)
                weight_job(("wo", c), wo_s[:, 4 * c:4 * c + 4, :], rows_of(wo)[:, 4 * c:4 * c + 4, :], 4, D)
            weight_job("gate", gate_s, rows_of(gate_t), KD, E)
            weight_job("sg", sg_s, rows_of(shared_gate), KD, FS)
            weight_job("su", su_s, rows_of(shared_up), KD, FS)
            weight_job("sd", sd_s, rows_of(shared_down), FSB, D)

        loaded, prepared = [0], [0]

        def load_weight():
            if loaded[0] == len(weight_jobs):
                return
            n = loaded[0]
            name, dst, src, rows, cols = weight_jobs[n]
            buf = weight_in[n % 2][:, 0:rows * cols].rearrange("p (k n) -> p k n", k=rows)
            mark["in", name] = load(in_weight[n % 2], buf, src, mark.get(("weight_free", n % 2)))
            loaded[0] += 1

        def prepare_weight():
            if prepared[0] == len(weight_jobs):
                return
            n = prepared[0]
            name, dst, src, rows, cols = weight_jobs[n]
            buf = weight_in[n % 2][:, 0:rows * cols].rearrange("p (k n) -> p k n", k=rows)
            mark[name] = mark["weight_free", n % 2] = split_sbuf(buf, dst, W_S, mark["in", name])
            prepared[0] += 1
            load_weight()

        def load_x(b):
            mark["x", b] = load(in_x[b % 2], x_in[b % 2][:, :, :],
                                x[b * T:(b + 1) * T, :].rearrange("(t p) d -> p t d", p=P), mark.get(("x1", b - 2)))

        def load_ctx(b):
            mark["ctx_in", b] = load(in_ctx, ctx_in[:, :, :], ctx_t[:, b * S:(b + 1) * S].rearrange("(k p) s -> p k s", p=P),
                                     mark.get(("ctx", b - 1)))

        def prepare_ctx(b):
            mark["ctx", b] = split_sbuf(ctx_in[:, :, :], ctx_s[b % 2], C_S, mark["ctx_in", b],
                                        mark.get(("key_pe", (b - 1) * KV - 1)))

        def load_mask(b):
            mark["mask_in", b] = load(in_mask, mask_in[:, :], mask[b:b + 1, :].broadcast_to([P, S]),
                                      mark.get(("mask", b - 1)))

        def prepare_mask(b):
            pool.wait(mark["mask_in", b], mark.get(("max", (b - 1) * KV - 1)))
            mark["mask", b] = pool.do(lambda e: e.tensor_scalar(mask_add[b % 2][:, :], mask_in[:, :], -1.0, MASKED,
                                                                ALU.add, ALU.mult), pool_mask)

        def layer_norm(src, dst, ready, free):
            dve.wait(ready, mark.get("rstd"))
            for t in range(TB):
                m = dve.do(lambda e, t=t: e.bn_stats(stats[:, t, :], src[:, t, :]), dve_stats)
            dve.wait(m)
            for t in range(TB):
                m = dve.do(lambda e, t=t: e.bn_aggr(mean_var[:, t, :], stats[:, t, :]), dve_stats)
            pool.wait(m, mark.get("normed_last"))
            m = pool.do(lambda e: e.tensor_scalar(var_eps[:, :], mean_var[:, :, 1], LN_EPS, 1.0, ALU.add, ALU.mult), pool_rstd)
            pool.wait(m)
            m = mark["rstd"] = pool.do(lambda e: e.tensor_tensor(rstd[:, :], var_eps[:, :], minus_half[:, :], ALU.pow), pool_rstd)

            def apply():
                dve.wait(m, *free)
                for t in range(TB):
                    r = dve.do(lambda e, t=t: e.tensor_scalar(dst[:, t, :], src[:, t, :], mean_var[:, t, 0:1], rstd[:, t:t + 1],
                                                              ALU.subtract, ALU.mult), dve_normed)
                mark["normed_last"] = r
                return r
            return apply

        def transpose_rows(src, dst, t, ready, free, scale):
            dstb = ps_fill[1]
            pe.wait(ready, bank_free.get("fill1"))
            for k in range(KD):
                m = pe.do(lambda e, k=k: e.transpose(dstb[:, k * P:(k + 1) * P], src[:, t, k * P:(k + 1) * P], ident[:, :]),
                          pe_fill if k == KD - 1 else None)
            act.wait(*free)
            r = split_psum(dstb[:, :].rearrange("p (k t) -> p k t", k=KD), dst[:, :, t * P:(t + 1) * P], scale, m)
            bank_free["fill1"] = r
            return r

        def query(i, h):
            b, g = divmod(i, KV)
            pe.wait(mark["xn_t", b], mark["wq", g // 2], bank_free.get("query"))
            n = (g * PAIR + h) * HD
            m = products(ps_query[:, h * T:(h + 1) * T],
                         [(wq_s[:, k, n:n + HD], xn_t[b % 2][:, k, :]) for k in range(KD)],
                         pe_query if h == PAIR - 1 else None)
            if h < PAIR - 1:
                return
            act.wait(mark.get(("score_pe", i - 1)))
            mark["query_pe", i] = m
            mark["query", i] = bank_free["query"] = split_psum(ps_query[:, :], q_t, 1.0 / (W_S * X_S), m)

        def key(i):
            b, g = divmod(i, KV)
            pe.wait(mark["ctx", b], mark["wk"], bank_free.get("fill0"))
            m = products(ps_fill[0][:, 0:S], [(wk_s[:, k, g * HD:(g + 1) * HD], ctx_s[b % 2][:, k, :]) for k in range(KC)], pe_key)
            mark["key_pe", i] = m
            act.wait(mark.get(("score_pe", i - 1)))
            mark["key", i] = bank_free["fill0"] = split_psum(ps_fill[0][:, 0:S], k_t, 1.0 / (W_S * C_S), m)

        def value(b, half, s):
            cols = slice(half * 512, (half + 1) * 512)
            pe.wait(mark["ctx", b], mark["wv"], bank_free.get("fill1"))
            m = products(ps_fill[1][:, :], [(ctx_s[b % 2][:, k, s * P:(s + 1) * P], wv_s[:, k, cols]) for k in range(KC)], pe_fill)
            act.wait(mark.get(("head_pe", (b - 1) * KV - 1)))
            n = b * SB + s
            mark["value", b, half, s] = bank_free["fill1"] = split_psum(
                ps_fill[1][:, :], v_s[b % 2][:, s, cols], None, m, vector_scale=value_scale[:, n:n + 1])

        def scores(i):
            pe.wait(mark["query", i], mark["key", i], bank_free.get("score"))
            for h in range(PAIR):
                for t in range(TB):
                    c = h * T + t * P
                    m = products(ps_score[h][:, t * S:(t + 1) * S], [(q_t[:, c:c + P], k_t)],
                                 pe_score if t == TB - 1 else None)
                mark["score_pe", i, h] = m
            mark["score_pe", i] = m

        def softmax_exp(i):
            b = i // KV
            dve.wait(mark["mask", b], mark.get(("trans_pe", i - 1)))
            for c in range(PAIR * TB):
                h, t = divmod(c, TB)
                dve.wait(mark["score_pe", i, h])
                m = dve.do(lambda e, c=c, h=h, t=t: e.tensor_tensor_reduce(
                    out=probs[:, c, :], in0=ps_score[h][:, t * S:(t + 1) * S], in1=mask_add[b % 2][:, :],
                    scale=-SCORE_SCALE, scalar=3e38, op0=ALU.add, op1=ALU.min, accum_out=neg_max[:, c:c + 1]), dve_max)
                act.wait(m)
                a = act.do(lambda e, c=c: e.activation(probs[:, c, :], probs[:, c, :], ACT.Exp, bias=neg_max[:, c:c + 1],
                                                       scale=-1.0, accum_out=prob_sum[:, c:c + 1]), act_exp)
            mark["max", i] = bank_free["score"] = m
            mark["exp", i] = a

        def softmax_norm(i):
            dve.wait(mark["exp", i], mark.get(("norm", i - 1)))
            r = dve.do(lambda e: e.reciprocal(prob_inv[:, :], prob_sum[:, :]), dve_inv)
            pool.wait(r)
            for c in range(PAIR * TB):
                m = pool.do(lambda e, c=c: e.tensor_scalar(probs[:, c, :], probs[:, c, :], prob_inv[:, c:c + 1], P_S,
                                                           ALU.mult, ALU.mult), pool_norm)
            mark["norm", i] = m

        def transpose_probs(i):
            pe.wait(mark["norm", i], bank_free.get("fill0"), bank_free.get("fill1"))
            ms = []
            for s in range(SB):
                for c in range(PAIR * TB):
                    m = pe.do(lambda e, s=s, c=c: e.transpose(ps_fill[s][:, c * P:(c + 1) * P], probs[:, c, s * P:(s + 1) * P],
                                                              ident[:, :]), pe_trans if c == PAIR * TB - 1 else None)
                ms.append(m)
            mark["trans_pe", i] = ms[-1]
            act.wait(mark.get(("head_pe", i - 1)))
            for s in range(SB):
                mark["probs", i] = bank_free[f"fill{s}"] = split_psum(ps_fill[s][:, :], p_t[:, s, :], 1.0, ms[s])

        def attend(i):
            b, g = divmod(i, KV)
            pe.wait(mark["probs", i], mark["value", b, g // 4, 0], mark["value", b, g // 4, 1], bank_free.get("head"))
            m = products(ps_head[:, :], [(v_s[b % 2][:, s, g * HD:(g + 1) * HD], p_t[:, s, :]) for s in range(SB)], pe_head)
            mark["head_pe", i] = m
            act.wait(mark.get(("out_pe", i - 1)))
            mark["head", i] = bank_free["head"] = split_psum(ps_head[:, :], o_t, 1.0 / P_S, m)

        def project(i):
            b, g = divmod(i, KV)
            pe.wait(mark["head", i], mark["wo", g // 2], bank_free.get("out") if g == 0 else None)
            for t in range(TB):
                m = products(ps_out[t][:, :], [(o_t[:, h * T + t * P:h * T + (t + 1) * P], wo_s[:, g * PAIR + h, :])
                                               for h in range(PAIR)],
                             pe_out if t == TB - 1 else None, first=g == 0, last=g == KV - 1)
            mark["out_pe", i] = m

        def residual(b):
            dve.wait(mark["out_pe", b * KV + KV - 1], mark["x", b], mark.get(("rows_out", b - 1)))
            for t in range(TB):
                m = dve.do(lambda e, t=t: e.scalar_tensor_tensor(x1[:, t, :], ps_out[t][:, :], 1.0 / (V_S * W_S),
                                                                 x_in[b % 2][:, t, :], ALU.mult, ALU.add), dve_residual)
            mark["x1", b] = bank_free["out"] = m

        def gate(b):
            pe.wait(mark["xn2_t", b], mark["gate"], bank_free.get("fill1"))
            for t in range(TB):
                m = products(ps_fill[1][:, t * E:(t + 1) * E],
                             [(xn2_t[:, k, t * P:(t + 1) * P], gate_s[:, k, :]) for k in range(KD)],
                             pe_fill if t == TB - 1 else None)
            act.wait(m)
            m = act.do(lambda e: e.activation(exp_neg[:, :, :], ps_fill[1][:, 0:TB * E].rearrange("p (t e) -> p t e", e=E),
                                              ACT.Exp, scale=-1.0 / (W_S * X_S)), act_fn)
            bank_free["fill1"] = mark["exp_neg", b] = m

        def chain(build_):
            m = dve.do(build_, dve_route)
            dve.wait(m)
            return m

        def choose(b):
            dve.wait(mark["exp_neg", b])
            chain(lambda e: e.tensor_scalar(exp_neg[:, :, :], exp_neg[:, :, :], 1.0, None, ALU.add))
            chain(lambda e: e.reciprocal(score[:, :, :], exp_neg[:, :, :]))
            mark["score_read", b] = chain(lambda e: e.tensor_tensor(
                biased[:, :, :], score[:, :, :], bias_row[:, :].unsqueeze(1).broadcast_to([P, TB, E]), ALU.add))
            flat = biased[:, :, :].rearrange("p t e -> p (t e)")
            for g in range(TB * GROUPS):
                m = dve.do(lambda e, g=g: e.max(group_top[:, g, :], flat[:, g * EPG:(g + 1) * EPG]), dve_route)
            dve.wait(m)
            top = group_top[:, :, :].rearrange("p (t g) k -> p t g k", t=TB)
            chain(lambda e: e.tensor_tensor(group_score[:, :, :], top[:, :, :, 0], top[:, :, :, 1], ALU.add))
            full = [P, TB, GROUPS, GROUPS]
            mine = group_score[:, :, :].unsqueeze(3).broadcast_to(full)
            other = group_score[:, :, :].unsqueeze(2).broadcast_to(full)
            dve.do(lambda e: e.tensor_tensor(beats[:, :, :, :], other, mine, ALU.is_gt))
            chain(lambda e: e.tensor_tensor(ties[:, :, :, :], other, mine, ALU.is_equal))
            chain(lambda e: e.tensor_tensor(ties[:, :, :, :], ties[:, :, :, :],
                                            lower[:, :, :].unsqueeze(1).broadcast_to(full), ALU.mult))
            chain(lambda e: e.tensor_tensor(beats[:, :, :, :], beats[:, :, :, :], ties[:, :, :, :], ALU.add))
            chain(lambda e: e.reduce_sum(group_rank[:, :, :], beats[:, :, :, :], AX.X))
            chain(lambda e: e.tensor_scalar(group_rank[:, :, :], group_rank[:, :, :], float(TOPG), None, ALU.is_lt))
            by_group = biased[:, :, :].rearrange("p t (g e) -> p (t g) e", g=GROUPS)
            chain(lambda e: e.tensor_tensor(by_group, by_group, group_rank[:, :, :].rearrange("p t g -> p (t g)")
                                            .unsqueeze(2).broadcast_to([P, TB * GROUPS, EPG]), ALU.mult))
            for t in range(TB):
                m = dve.do(lambda e, t=t: e.max(top8[:, t, :], biased[:, t, :]), dve_route)
            dve.wait(m)
            for t in range(TB):
                m = dve.do(lambda e, t=t: e.max_index(top8_at[:, t, :], top8[:, t, :], biased[:, t, :]), dve_route)
            dve.wait(m)
            chain(lambda e: e.tensor_copy(chosen[:, :, :], top8_at[:, :, 0:TOPK]))
            for t in range(TB):
                m = dve.do(lambda e, t=t: e.tensor_tensor(
                    one_hot[:, t, :, :], expert_no[:, :].unsqueeze(1).broadcast_to([P, TOPK, E]),
                    chosen[:, t, :].unsqueeze(2).broadcast_to([P, TOPK, E]), ALU.is_equal), dve_route)
            dve.wait(m, mark.get(("rank_pe", b - 1)))

            def count_uses(e):
                with nc.allow_low_precision(reason="0 and 1 are exact in float16"):
                    return e.reduce_sum(uses[:, :, :], one_hot[:, :, :, :].rearrange("p t k e -> p t e k"), AX.X)
            mark["uses", b] = dve.do(count_uses, dve_route)
            pick(score, weight)
            chain(lambda e: e.reduce_sum(weight_sum[:, :], weight[:, :, :], AX.X))
            chain(lambda e: e.tensor_scalar(weight_sum[:, :], weight_sum[:, :], 1e-20, None, ALU.add))
            chain(lambda e: e.reciprocal(weight_inv[:, :], weight_sum[:, :]))
            chain(lambda e: e.tensor_scalar(weight_inv[:, :], weight_inv[:, :], ROUTE_SCALE, None, ALU.mult))
            dve.wait(mark.get(("scattered", b - 2)))
            mark["weight", b] = dve.do(lambda e: e.tensor_tensor(
                entry[b % 2][:, :, :, 1].bitcast(F32), weight[:, :, :], weight_inv[:, :].unsqueeze(2).broadcast_to([P, TB, TOPK]),
                ALU.mult), dve_route)

        def pick(table_, dst):
            for t in range(TB):
                m = dve.do(lambda e, t=t: e.tensor_tensor(
                    picked[:, t, :, :], one_hot[:, t, :, :], table_[:, t, :].unsqueeze(1).broadcast_to([P, TOPK, E]), ALU.mult),
                    dve_route)
            dve.wait(m)
            chain(lambda e: e.reduce_sum(dst[:, :, :], picked[:, :, :, :], AX.X))

        def rank(b):
            ps = ps_fill[1]
            pe.wait(mark["uses", b], bank_free.get("fill1"))
            for t in range(TB):
                for u in range(t + 1):
                    pe.do(lambda e, t=t, u=u: e.matmul(ps[:, t * E:(t + 1) * E], (earlier if u == t else ones)[:, :],
                                                       uses[:, u, :], start=u == 0, stop=u == t))
            for u in range(TB):
                m = pe.do(lambda e, u=u: e.matmul(ps[:, TB * E:(TB + 1) * E], ones[:, :], uses[:, u, :], start=u == 0,
                                                  stop=u == TB - 1), pe_fill if u == TB - 1 else None)
            mark["rank_pe", b] = m

        def place(b):
            ps = ps_fill[1]
            dve.wait(mark["rank_pe", b])
            chain(lambda e: e.tensor_tensor(position[:, :, :], ps[:, 0:TB * E].rearrange("p (t e) -> p t e", e=E),
                                            taken[:, :].unsqueeze(1).broadcast_to([P, TB, E]), ALU.add))
            bank_free["fill1"] = chain(lambda e: e.tensor_tensor(taken[:, :], ps[:, TB * E:(TB + 1) * E], taken[:, :], ALU.add))
            pick(position, my_position)
            chain(lambda e: e.scalar_tensor_tensor(slot_f[:, :, :], my_position[:, :, :], float(E), chosen[:, :, :],
                                                   ALU.mult, ALU.add))
            mark["slot", b] = dve.do(lambda e: e.tensor_copy(slot_at[b % 2][:, :, :], slot_f[:, :, :]), dve_route)

        def record(b):
            pool.wait(mark.get(("scattered", b - 2)))
            pool.do(lambda e: e.iota(entry[b % 2][:, :, :, 0], pattern=[[P, TB], [0, TOPK]], base=b * T, channel_multiplier=1),
                    pool_entry)
            pool.wait((pool_entry, pool_entry.value), mark["weight", b], mark["slot", b], mark["blank"])
            for t in range(TB):
                for k in range(TOPK):
                    m = pool.do(lambda e, t=t, k=k: e.indirect_dma_start(
                        slot_table, bass.IndirectOffsetOnAxis(ap=slot_at[b % 2][:, t, k:k + 1], axis=0),
                        entry[b % 2][:, t, k, :], None, bounds_check=CAP * E - 1, oob_is_err=False), scattered[b % 2], 16)
            mark["scattered", b] = m

        def swiglu(g_psum, u_psum, dst, scale, ready, free):
            k = 1.0 / (W_S * X_S)
            act.wait(ready, mark.get("glu_last"))
            m = act.do(lambda e: e.activation(tanh_g[:, :], g_psum, ACT.Tanh, scale=0.5 * k), act_fn)
            dve.wait(m)
            m = dve.do(lambda e: e.scalar_tensor_tensor(gated[:, :], tanh_g[:, :], 1.0, g_psum, ALU.add, ALU.mult), dve_glu)
            dve.wait(m, *free)
            m = dve.do(lambda e: e.scalar_tensor_tensor(dst, gated[:, :], 0.5 * k * k * scale, u_psum, ALU.mult, ALU.mult), dve_glu)
            mark["glu_last"] = m
            return m

        def shared_up_part(b, f):
            pe.wait(mark["xn2_t", b], mark["sg"], mark["su"], bank_free.get("fill1"))
            for n, w in enumerate((sg_s, su_s)):
                m = products(ps_fill[1][:, n * T:(n + 1) * T], [(w[:, k, f * P:(f + 1) * P], xn2_t[:, k, :]) for k in range(KD)],
                             pe_fill if n else None)
            mark["xn2_t_read", b] = m
            m = swiglu(ps_fill[1][:, 0:T], ps_fill[1][:, T:2 * T], hidden[:, :], HS_S, m, [mark.get("hidden_read")])
            bank_free["fill1"] = m
            pool.wait(m, mark.get(("shared_pe", b - 1)))
            m = pool.do(lambda e: e.tensor_scalar(h_t.hi[:, f, :], hidden[:, :], 1.0, 1.0, ALU.mult, ALU.mult), pool_hi)
            pool.wait(m)
            mark["hidden", b] = mark["hidden_read"] = pool.do(
                lambda e: e.tensor_tensor(h_t.lo[:, f, :], hidden[:, :], h_t.hi[:, f, :], ALU.subtract), pool_hi)

        def shared_down_part(b, t):
            pe.wait(mark["hidden", b], mark["sd"], bank_free.get("fill1"))
            m = products(ps_fill[1][:, :], [(h_t[:, f, t * P:(t + 1) * P], sd_s[:, f, :]) for f in range(FSB)], pe_fill)
            mark["shared_pe", b] = m
            dve.wait(m, mark["x1", b])
            m = bank_free["fill1"] = dve.do(lambda e: e.scalar_tensor_tensor(
                x1[:, t, :], ps_fill[1][:, :], 1.0 / (HS_S * W_S), x1[:, t, :], ALU.mult, ALU.add), dve_residual)
            r = b * T + t * P
            mark["rows_out", b] = load(out_rows, out[r:r + P, :], x1[:, t, :], m)

        norms = {}

        def before_x(b):
            norms["x"] = layer_norm(x_in[b % 2], normed, mark["x", b], [mark.get(("xn_t", b - 1))])

        def apply_x(b):
            mark["normed", b] = norms["x"]()

        def x_t(b, t):
            mark["xn_t", b] = transpose_rows(normed, xn_t[b % 2], t, mark["normed", b],
                                             [mark.get(("query_pe", (b - 1) * KV - 1))], X_S)

        def before_xn2(b):
            norms["x1"] = layer_norm(x1, xn2, mark["x1", b],
                                     [mark.get(("xn2_out", b - 1)), mark.get(("xn2_t", b - 1)), mark["blank"]])

        def apply_xn2(b):
            m = mark["xn2", b] = norms["x1"]()
            mark["xn2_out", b] = load(out_xn2, xn2_rows[b * T:(b + 1) * T, :].rearrange("(t p) d -> p t d", p=P),
                                      xn2[:, :, :], m)

        def xn2_transposed(b, t):
            mark["xn2_t", b] = transpose_rows(xn2, xn2_t, t, mark["xn2", b], [mark.get(("xn2_t_read", b - 1))], X_S)

        def fillers(b, j):
            ahead, behind = b + 1 < B, 0 <= b - 1
            a, z = b + 1, b - 1
            none = lambda: None
            table_ = {
                0: [ahead and (lambda: value(a, 0, 0)), ahead and (lambda: value(a, 0, 1))],
                1: [ahead and (lambda: value(a, 1, 0)), ahead and (lambda: value(a, 1, 1))],
                2: [behind and (lambda: xn2_transposed(z, 0)), behind and (lambda: xn2_transposed(z, 1))],
                3: [behind and (lambda: gate(z)), behind and (lambda: shared_up_part(z, 0))],
                4: [ahead and (lambda: x_t(a, 0)), behind and (lambda: shared_up_part(z, 1))],
                5: [ahead and (lambda: x_t(a, 1)), behind and (lambda: shared_up_part(z, 2))],
                6: [behind and (lambda: (rank(z), place(z))), behind and (lambda: shared_up_part(z, 3))],
                7: [behind and (lambda: shared_down_part(z, 0)), behind and (lambda: shared_down_part(z, 1))],
            }
            return [f or none for f in table_[j]]

        def side_work(b, j):
            ahead, behind = b + 1 < B, 0 <= b - 1
            if j == 1:
                if behind:
                    before_xn2(b - 1)
                    apply_xn2(b - 1)
                if ahead:
                    load_x(b + 1)
                    load_mask(b + 1)
            if j == 2 and ahead:
                prepare_mask(b + 1)
                before_x(b + 1)
            if j == 3:
                if ahead:
                    apply_x(b + 1)
                if behind:
                    choose(b - 1)
            if j == 4 and b + 2 < B:
                load_ctx(b + 2)
            if j == 7:
                if behind:
                    record(b - 1)
                if b + 2 < B:
                    prepare_ctx(b + 2)

        def prologue():
            plan_weights()
            load_ctx(0)
            load_weight()
            load_x(0)
            load_weight()
            load_mask(0)
            constants()
            blank_rows()
            prepare_ctx(0)
            load_ctx(1)
            prepare_weight()
            before_x(0)
            apply_x(0)
            for t in range(TB):
                x_t(0, t)
            key(0)
            prepare_weight()
            for h in range(PAIR):
                query(0, h)
            prepare_mask(0)
            prepare_ctx(1)

        prepare_at = {0: 2, 2: 2, 4: 2, 6: 2, 7: 1, 8: 1, 9: 1}

        def attention():
            for i in range(TURNS + 1):
                b, j = divmod(i, KV)
                if i < TURNS:
                    scores(i)
                    softmax_exp(i)
                if i == 0:
                    prepare_weight()
                if i == 0:
                    for half in range(2):
                        for s in range(SB):
                            value(0, half, s)
                if i + 1 < TURNS:
                    query(i + 1, 0)
                if i:
                    attend(i - 1)
                if i < TURNS:
                    softmax_norm(i)
                first, second = fillers(b, j) if i < TURNS else (lambda: None,) * 2
                first()
                if i + 1 < TURNS:
                    query(i + 1, 1)
                    key(i + 1)
                second()
                if i:
                    project(i - 1)
                for _ in range(prepare_at.get(i, 0)):
                    prepare_weight()
                if i < TURNS:
                    side_work(b, j)
                    transpose_probs(i)
                if i and j == 0:
                    residual(b - 1)

        def expert_views(n):
            w = expert_in[n % AHEAD]
            up = w[:, 0:KD * 2 * F].rearrange("p (k n) -> p k n", k=KD)
            down = w[:, KD * 2 * F:].rearrange("p (k n) -> p k n", k=FB)
            return up, down

        def load_expert(e_):
            up, down = expert_views(e_)
            after = [mark.get(("expert_split", e_ - AHEAD)), mark["query_pe", TURNS - 1], mark["key_pe", TURNS - 1]]
            sig = in_expert[e_ % AHEAD]
            load(sig, up[:, :, 0:F], w1[e_].rearrange("(p k) n -> p k n", p=P), *after)
            load(sig, up[:, :, F:2 * F], w3[e_].rearrange("(p k) n -> p k n", p=P))
            mark["expert_in", e_] = load(sig, down, w2[e_].rearrange("(p k) n -> p k n", p=P))

        def prepare_expert(e_, part):
            src, dst = expert_in[e_ % AHEAD], expert_w[e_ % AHEAD]
            third = EW // 3
            at = slice(part * third, (part + 1) * third)
            free = [mark.get(("expert_y_pe", e_ - AHEAD)), mark["out_pe", TURNS - 1]]
            if part < 2:
                act.wait(mark["expert_in", e_], *free)
                m = act.do(lambda e: e.activation(dst.hi[:, at], src[:, at], ACT.Copy, scale=W_S), act_hi)
            else:
                pool.wait(mark["expert_in", e_], *free)
                m = pool.do(lambda e: e.tensor_scalar(dst.hi[:, at], src[:, at], W_S, 1.0, ALU.mult, ALU.mult), pool_hi)
            dve.wait(mark["expert_in", e_], m, *free)
            mark["expert_split", e_] = dve.do(lambda e: e.scalar_tensor_tensor(
                dst.lo[:, at], src[:, at], W_S, dst.hi[:, at], ALU.mult, ALU.subtract), dve_lo)

        def load_table():
            m = load(in_table, table[:, :, :].rearrange("p e c -> p (e c)"), slot_table.rearrange("(p e) c -> p (e c)", e=E),
                     mark["scattered", B - 1], mark["scattered", B - 2])
            dve.wait(m)
            pool.wait(m)
            mark["slot_weight"] = dve.do(lambda e: e.tensor_scalar(slot_weight[:, :], table[:, :, 1].bitcast(F32),
                                                                   1.0 / (HE_S * W_S), None, ALU.mult), dve_route)
            act.wait(mark["slot_weight"])

        def gather(e_):
            pool.wait(mark.get(("rows_pe", e_ - 3)), mark["xn2_out", B - 1], mark["x1", B - 1], mark["x1", B - 2])
            mark["gathered", e_] = pool.do(lambda e: e.indirect_dma_start(
                rows_in[e_ % 3], None, xn2_rows, bass.IndirectOffsetOnAxis(ap=table[:, e_, 0:1], axis=0),
                bounds_check=N + CAP - 1, oob_is_err=True), gathered[e_ % 3], 16)

        def expert_rows(e_):
            rows = rows_in[e_ % 3].rearrange("c (p k) -> c k p", k=KD)
            ps = ps_fill[e_ % 2]
            pe.wait(mark["gathered", e_], bank_free.get(f"fill{e_ % 2}"))
            for k in range(KD):
                m = pe.do(lambda e, k=k: e.transpose(ps[:, k * P:(k + 1) * P], rows[:, k, :], ident[:, :]),
                          pe_fill if k == KD - 1 else None)
            mark["rows_pe", e_] = m
            act.wait(mark.get(("expert_up_pe", e_ - 2)), mark["query_pe", TURNS - 1])
            mark["rows_t", e_] = bank_free[f"fill{e_ % 2}"] = split_psum(
                ps[:, :].rearrange("p (k c) -> p k c", k=KD), rows_t[e_ % 2][:, :, 0:P], X_S, m)

        def expert_up(e_):
            ps = ps_score[e_ % 2]
            w = expert_w[e_ % AHEAD][:, 0:KD * 2 * F]
            pe.wait(mark["rows_t", e_], mark["expert_split", e_], bank_free.get(f"up{e_ % 2}"), bank_free.get("score"))
            m = products(ps[:, :], [(rows_t[e_ % 2][:, k, 0:P], w[:, k * 2 * F:(k + 1) * 2 * F]) for k in range(KD)], pe_score)
            mark["expert_up_pe", e_] = m
            mark["expert_h", e_] = bank_free[f"up{e_ % 2}"] = swiglu(
                ps[:, 0:F], ps[:, F:2 * F], expert_h, HE_S, m, [mark.get(("expert_ht_pe", e_ - 1)), mark["xn_t", B - 1]])

        def expert_hidden(e_):
            cols = expert_h.rearrange("c (p f) -> c f p", f=FB)
            ps = (ps_head, ps_query)[e_ % 2]
            pe.wait(mark["expert_h", e_], bank_free.get(("head", "query")[e_ % 2]))
            for f in range(FB):
                m = pe.do(lambda e, f=f: e.transpose(ps[:, f * P:(f + 1) * P], cols[:, f, :], ident[:, :]),
                          pe_trans if f == FB - 1 else None)
            mark["expert_ht_pe", e_] = m
            act.wait(mark.get(("expert_y_pe", e_ - 2)), mark[("shared_pe", B - 1)])
            mark["expert_ht", e_] = bank_free[("head", "query")[e_ % 2]] = split_psum(
                ps[:, 0:FB * P].rearrange("p (f c) -> p f c", f=FB), expert_h_t[e_ % 2], 1.0, m)

        def expert_down(e_):
            ps = ps_out[e_ % 2]
            w = expert_w[e_ % AHEAD][:, KD * 2 * F:]
            pe.wait(mark["expert_ht", e_], bank_free.get(f"y{e_ % 2}"), bank_free.get("out"))
            m = products(ps[:, :], [(expert_h_t[e_ % 2][:, f, :], w[:, f * D:(f + 1) * D]) for f in range(FB)], pe_out)
            mark["expert_y_pe", e_] = m
            act.wait(m, mark.get(("added", e_ - 4)), mark["sd"])
            m = bank_free[f"y{e_ % 2}"] = act.do(lambda e: e.activation(
                expert_y[e_ % 4], ps[:, :], ACT.Copy, scale=slot_weight[:, e_:e_ + 1]), act_y)
            pool.wait(m, mark.get(("added", e_ - 1)), mark["rows_out", B - 1])
            mark["added", e_] = pool.do(lambda e: e.indirect_dma_start(
                out, bass.IndirectOffsetOnAxis(ap=table[:, e_, 0:1], axis=0), expert_y[e_ % 4], None,
                bounds_check=N + CAP - 1, oob_is_err=True, compute_op=ALU.add), added, 16)

        def tail():
            z = B - 1
            for e_ in range(AHEAD):
                load_expert(e_)
            before_xn2(z)
            apply_xn2(z)
            for t in range(TB):
                xn2_transposed(z, t)
            gate(z)
            choose(z)
            shared_up_part(z, 0)
            rank(z)
            place(z)
            record(z)
            load_table()
            for e_ in range(3):
                gather(e_)
            for f in range(1, FSB):
                shared_up_part(z, f)
            for e_ in range(2):
                for part in range(3):
                    prepare_expert(e_, part)
                load_expert(e_ + AHEAD)
            for t in range(TB):
                shared_down_part(z, t)

        def experts():
            for e_ in range(2):
                expert_rows(e_)
                gather(e_ + 3)
            for e_ in range(E + 1):
                if e_ < E:
                    expert_up(e_)
                if e_ >= 1:
                    expert_down(e_ - 1)
                if e_ + 2 < E:
                    prepare_expert(e_ + 2, 0)
                if e_ < E:
                    expert_hidden(e_)
                if e_ + 2 < E:
                    prepare_expert(e_ + 2, 1)
                    prepare_expert(e_ + 2, 2)
                    expert_rows(e_ + 2)
                    if e_ + 5 < E:
                        gather(e_ + 5)
                    if e_ + 2 + AHEAD < E:
                        load_expert(e_ + 2 + AHEAD)
            pool.wait(mark["added", E - 1])
            sync.wait(mark["rows_out", B - 1], mark["xn2_out", B - 1], mark["blank"])

        prologue()
        attention()
        tail()
        experts()

        block = stack.enter_context(nc.Block())
        block.sync(sync.run)
        block.gpsimd(pool.run)
        block.scalar(act.run)
        block.vector(dve.run)
        block.tensor(pe.run)


def kernel(x, ctx_1024, mask_BxS2_bf1, L0_xattn_Wq, L0_xattn_Wk, L0_xattn_Wv, L0_xattn_Wo, L0_ffn_gate_w, L0_ffn_gate_bias,
           L0_ffn_w1, L0_ffn_w2, L0_ffn_w3, L0_ffn_shared_gate, L0_ffn_shared_up, L0_ffn_shared_down):
    import concourse.bacc as bacc
    from concourse.bass_utils import run_bass_kernel_spmd

    mask = np.ascontiguousarray(mask_BxS2_bf1).view(np.uint8)
    arrays = {
        "x": np.asarray(x).reshape(N, D),
        "ctx_t": np.asarray(ctx_1024).reshape(B * S, DC).T,
        "mask": mask,
        "mask_cols": mask.reshape(B * SB, P).T,
        "wq": L0_xattn_Wq, "wk": L0_xattn_Wk, "wv": L0_xattn_Wv, "wo": L0_xattn_Wo,
        "gate_t": np.asarray(L0_ffn_gate_w).T,
        "gate_bias": np.asarray(L0_ffn_gate_bias).reshape(1, E),
        "w1": L0_ffn_w1, "w2": L0_ffn_w2, "w3": L0_ffn_w3,
        "shared_gate": L0_ffn_shared_gate, "shared_up": L0_ffn_shared_up, "shared_down": L0_ffn_shared_down,
    }
    arrays = {k: np.ascontiguousarray(a) for k, a in arrays.items()}
    nc = bacc.Bacc("TRN2", target_bir_lowering=False, num_devices=1)
    args = [nc.dram_tensor(k, a.shape, mybir.dt.from_np(a.dtype), kind="ExternalInput").ap() for k, a in arrays.items()]
    out = nc.dram_tensor("out_rows_dram", (N + CAP, D), F32, kind="ExternalOutput").ap()
    build(nc, *args, out)
    got = run_bass_kernel_spmd(nc, [arrays], core_ids=[0])
    return got.results[0]["out_rows_dram"][:N].reshape(B, T, D)
```

```python
from collections import deque
from contextlib import ExitStack

import numpy as np

import concourse.bass as bass
import concourse.mybir as mybir

F32, F16, U32, U8 = mybir.dt.float32, mybir.dt.float16, mybir.dt.uint32, mybir.dt.uint8
ALU = mybir.AluOpType
ACT = mybir.ActivationFunctionType
AX = mybir.AxisListType

P = 128
B, T, D = 16, 256, 512
S, DC = 256, 256
HEADS, KV, HD = 16, 8, 128
PAIR = HEADS // KV
E, TOPK, GROUPS, TOPG = 32, 4, 4, 2
F, FS = 256, 512
ROUTE_SCALE = 2.0
CAP = 2 * (2 * 256 * TOPK // E)
N = B * T
EPG = E // GROUPS

TB, SB, KD, KC, FB, FSB = T // P, S // P, D // P, DC // P, F // P, FS // P
TURNS = B * KV
assert CAP == P

W_S = 64.0
X_S = 64.0
C_S = 16.0
V_S = 16.0
P_S = 1024.0
HS_S = 64.0
HE_S = 16.0
MASKED = 1e30
LN_EPS = 1e-5
SCORE_SCALE = 1.0 / float(np.sqrt(np.float32(HD)))


class Signal:

    def __init__(self, handle):
        self.handle, self.value = handle, 0


class Queue:

    def __init__(self):
        self.steps, self.seen = [], {}

    def wait(self, *marks):
        for mark in marks:
            if mark is None:
                continue
            signal, value = mark
            if self.seen.get(id(signal), 0) < value:
                self.seen[id(signal)] = value
                self.steps.append(lambda eng, h=signal.handle, v=value: eng.wait_ge(h, v))

    def do(self, build, signal=None, by=1):
        if signal is None:
            self.steps.append(build)
            return None
        self.steps.append(lambda eng, h=signal.handle: build(eng).then_inc(h, by))
        signal.value += by
        return (signal, signal.value)

    def run(self, eng):
        for step in self.steps:
            step(eng)


class Split:

    def __init__(self, hi, lo):
        self.hi, self.lo = hi, lo

    def __getitem__(self, at):
        return Split(self.hi[at], self.lo[at])


def build(nc, x, ctx_t, mask, mask_cols, wq, wk, wv, wo, gate_t, gate_bias, w1, w2, w3,
          shared_gate, shared_up, shared_down, out):
    stack = ExitStack()
    with stack:
        def sbuf(name, shape, dt=F32):
            return stack.enter_context(nc.sbuf_tensor(name, [P] + list(shape), dt))

        def split(name, shape):
            both = sbuf(name, [2] + list(shape), F16)
            if len(shape) == 1:
                return Split(both[:, 0, :], both[:, 1, :])
            return Split(both[:, 0], both[:, 1])

        def signal(name):
            return Signal(stack.enter_context(nc.semaphore(name)))

        xn2_rows = nc.dram_tensor("xn2_rows", (N + CAP, D), F32, kind="Internal").ap()
        slot_table = nc.dram_tensor("slot_table", (CAP * E, 2), U32, kind="Internal").ap()

        sizes = [(KC, KV * HD), (KC, KV * HD), (KD, HEADS * HD), (HEADS, D)]
        attention_w = sbuf("attention_w", [sum(2 * k * n for k, n in sizes)], F16)

        def carve():
            at = 0
            for k, n in sizes:
                yield Split(*(attention_w[:, at + i * k * n:at + (i + 1) * k * n].rearrange("p (k n) -> p k n", k=k)
                              for i in (0, 1)))
                at += 2 * k * n
        wv_s, wk_s, wq_s, wo_s = carve()
        sg_s = split("sg_s", [KD, FS])
        su_s = split("su_s", [KD, FS])
        sd_s = split("sd_s", [FSB, D])
        gate_s = split("gate_s", [KD, E])
        CHUNK = 2048
        weight_in = [sbuf(f"weight_in{n}", [CHUNK]) for n in range(2)]

        x_in = [sbuf(f"x_in{n}", [TB, D]) for n in range(2)]
        normed = sbuf("normed", [TB, D])
        xn_t = [split(f"xn_t{n}", [KD, T]) for n in range(2)]
        ctx_in = sbuf("ctx_in", [KC, S])
        ctx_s = [split(f"ctx_s{n}", [KC, S]) for n in range(2)]
        mask_in = sbuf("mask_in", [S], U8)
        mask_add = [sbuf(f"mask_add{n}", [S]) for n in range(2)]
        mask_cols_in = sbuf("mask_cols_in", [B * SB], U8)
        value_scale = sbuf("value_scale", [B * SB])
        v_s = [split(f"v_s{n}", [SB, KV * HD]) for n in range(2)]
        q_t = split("q_t", [PAIR * T])
        k_t = split("k_t", [S])
        probs = sbuf("probs", [PAIR * TB, S])
        neg_max = sbuf("neg_max", [PAIR * TB])
        prob_sum = sbuf("prob_sum", [PAIR * TB])
        prob_inv = sbuf("prob_inv", [PAIR * TB])
        prob_scale = sbuf("prob_scale", [PAIR * TB])
        p_rows = sbuf("p_rows", [2, PAIR * TB, S], F16)
        p_both = sbuf("p_both", [2, PAIR * TB, SB, P], F16)
        p_t = [Split(p_both[:, 0, :, s, :], p_both[:, 1, :, s, :]) for s in range(SB)]
        o_t = split("o_t", [PAIR * T])
        stats = sbuf("stats", [TB, 6])
        mean_var = sbuf("mean_var", [TB, 2])
        var_eps = sbuf("var_eps", [TB])
        rstd = sbuf("rstd", [TB])
        minus_half = sbuf("minus_half", [TB])
        x1 = sbuf("x1", [TB, D])
        xn2 = sbuf("xn2", [TB, D])
        xn2_t = split("xn2_t", [KD, T])
        tanh_g = sbuf("tanh_g", [T])
        gated = sbuf("gated", [T])
        hidden = sbuf("hidden", [T])
        h_t = split("h_t", [FSB, T])
        bias_row = sbuf("bias_row", [E])
        exp_neg = sbuf("exp_neg", [TB, E])
        score = sbuf("score", [TB, E])
        biased = sbuf("biased", [TB, E])
        group_top = sbuf("group_top", [TB * GROUPS, 8])
        group_score = sbuf("group_score", [TB, GROUPS])
        beats = sbuf("beats", [TB, GROUPS, GROUPS])
        ties = sbuf("ties", [TB, GROUPS, GROUPS])
        lower = sbuf("lower", [GROUPS, GROUPS])
        group_rank = sbuf("group_rank", [TB, GROUPS])
        top8 = sbuf("top8", [TB, 8])
        top8_at = sbuf("top8_at", [TB, 8], U32)
        chosen = sbuf("chosen", [TB, TOPK])
        expert_no = sbuf("expert_no", [E])
        one_hot = sbuf("one_hot", [TB, TOPK, E])
        picked = sbuf("picked", [TB, TOPK, E])
        weight = sbuf("weight", [TB, TOPK])
        weight_sum = sbuf("weight_sum", [TB])
        weight_inv = sbuf("weight_inv", [TB])
        uses = sbuf("uses", [TB, E], F16)
        earlier = sbuf("earlier", [P], F16)
        ones = sbuf("ones", [P], F16)
        taken = sbuf("taken", [E])
        position = sbuf("position", [TB, E])
        my_position = sbuf("my_position", [TB, TOPK])
        slot_f = sbuf("slot_f", [TB, TOPK])
        slot_at = [sbuf(f"slot_at{n}", [TB, TOPK], U32) for n in range(2)]
        entry = [sbuf(f"entry{n}", [TB, TOPK, 2], U32) for n in range(2)]
        ident = sbuf("ident", [P])
        blank = sbuf("blank", [E, 2], U32)

        EW = KD * 2 * F + FB * D
        AHEAD = 3
        expert_in = [attention_w[:, 2 * n * EW:2 * (n + 1) * EW].bitcast(F32) for n in range(AHEAD)]
        expert_w = [Split(attention_w[:, 2 * n * EW:(2 * n + 1) * EW], attention_w[:, (2 * n + 1) * EW:(2 * n + 2) * EW])
                    for n in range(AHEAD, 2 * AHEAD)]
        rows_in = [x_in[0][:, 0, :], x_in[0][:, 1, :], x_in[1][:, 0, :]]
        rows_t = xn_t
        table = sbuf("table", [E, 2], U32)
        slot_weight = sbuf("slot_weight", [E])
        expert_h = normed[:, 0, 0:F]
        expert_h_t = [h_t[:, 0:FB, 0:P], h_t[:, FB:2 * FB, 0:P]]
        expert_y = [weight_in[n // 2][:, (n % 2) * D:(n % 2 + 1) * D] for n in range(4)]

        def bank(name):
            return stack.enter_context(nc.psum_tensor(name, [P, 512], F32))

        ps_score = [bank("ps_score0"), bank("ps_score1")]
        ps_fill = [bank("ps_fill0"), bank("ps_fill1")]
        ps_head = bank("ps_head")
        ps_query = bank("ps_query")
        ps_out = [bank("ps_out0"), bank("ps_out1")]
        bank_free = {}

        use = [1]

        def filler_bank():
            return f"fill{use[0]}", ps_fill[use[0]]

        sync, pool, act, dve, pe = (Queue() for _ in range(5))

        consts = signal("consts")
        pe_query, pe_key, pe_score, pe_trans = (signal(n) for n in ("pe_query", "pe_key", "pe_score", "pe_trans"))
        pe_head, pe_out, pe_fill = signal("pe_head"), signal("pe_out"), signal("pe_fill")
        act_hi, dve_lo = signal("act_hi"), signal("dve_lo")
        pool_hi = signal("pool_hi")
        dve_max, act_exp, dve_inv, pool_norm = (signal(n) for n in ("dve_max", "act_exp", "dve_inv", "pool_norm"))
        dve_stats, pool_rstd, dve_normed = signal("dve_stats"), signal("pool_rstd"), signal("dve_normed")
        dve_residual, act_fn, dve_glu = signal("dve_residual"), signal("act_fn"), signal("dve_glu")
        dve_route, pool_entry, pool_mask = signal("dve_route"), signal("pool_entry"), signal("pool_mask")
        act_y = signal("act_y")
        in_weight = [signal(f"in_weight{n}") for n in range(2)]
        in_x = [signal(f"in_x{n}") for n in range(2)]
        in_ctx, in_mask, in_const = signal("in_ctx"), signal("in_mask"), signal("in_const")
        out_rows, out_xn2 = signal("out_rows"), signal("out_xn2")
        in_table = signal("in_table")
        scattered = [signal(f"scattered{n}") for n in range(2)]
        gathered = [signal(f"gathered{n}") for n in range(3)]
        in_expert = [signal(f"in_expert{n}") for n in range(AHEAD)]
        added = signal("added")
        dve_low, turned = signal("dve_low"), signal("turned")
        out_blank = signal("out_blank")

        mark = {}

        def load(signal_, dst, src, *after):
            sync.wait(*after)
            return sync.do(lambda e: e.dma_start(dst, src), signal_, 16)

        def product(dst, a, b, first, last):
            pe.do(lambda e: e.matmul(dst, a.hi, b.hi, start=first, stop=False))
            pe.do(lambda e: e.matmul(dst, a.hi, b.lo, start=False, stop=False))
            final = lambda e: e.matmul(dst, a.lo, b.hi, start=False, stop=last)
            return final

        def products(dst, pairs, sig=None, first=True, last=True):
            for n, (a, b) in enumerate(pairs):
                final = product(dst, a, b, first and n == 0, last and n == len(pairs) - 1)
                end = n == len(pairs) - 1
                m = pe.do(final, sig if end else None)
            return m

        def split_psum(src, dst, scale, ready, vector_scale=None):
            s = scale if vector_scale is None else vector_scale
            act.wait(ready)
            hi = act.do(lambda e: e.activation(dst.hi, src, ACT.Copy, scale=s), act_hi)
            dve.wait(hi)
            return dve.do(lambda e: e.scalar_tensor_tensor(dst.lo, src, s, dst.hi, ALU.mult, ALU.subtract), dve_lo)

        def split_sbuf(src, dst, scale, ready, free=None):
            pool.wait(ready, free)
            hi = pool.do(lambda e: e.tensor_scalar(dst.hi, src, scale, 1.0, ALU.mult, ALU.mult), pool_hi)
            dve.wait(ready, free, hi)
            return dve.do(lambda e: e.scalar_tensor_tensor(dst.lo, src, scale, dst.hi, ALU.mult, ALU.subtract), dve_lo)

        side = deque()

        def begin(name, pieces):
            side.append((name, pieces))

        def piece():
            if side and next(side[0][1], "end") == "end":
                side.popleft()
                piece()

        def finish(name):
            while any(n == name for n, _ in side):
                _, pieces = side.popleft()
                for _ in pieces:
                    pass

        def constants():
            pool.do(lambda e: e.memset(ident[:, :], 0.0), consts)
            pool.do(lambda e: e.memset(earlier[:, :], 1.0), consts)
            pool.do(lambda e: e.memset(lower[:, :, :], 1.0), consts)
            pool.do(lambda e: e.memset(xn2[:, 0, :], 0.0), consts)
            pool.do(lambda e: e.memset(blank[:, :, 1], 0), consts)
            m = pool.do(lambda e: e.memset(minus_half[:, :], -0.5), consts)
            pool.wait(m)
            pool.do(lambda e: e.affine_select(out=ident[:, :], in_=ident[:, :], compare_op=ALU.not_equal, fill=1.0,
                                              base=0, pattern=[[-1, P]], channel_multiplier=1), consts)
            pool.do(lambda e: e.affine_select(out=earlier[:, :], in_=earlier[:, :], compare_op=ALU.is_gt, fill=0.0,
                                              base=0, pattern=[[1, P]], channel_multiplier=-1), consts)
            pool.do(lambda e: e.affine_select(out=lower[:, :, :], in_=lower[:, :, :], compare_op=ALU.is_gt, fill=0.0,
                                              base=0, pattern=[[1, GROUPS], [-1, GROUPS]], channel_multiplier=0), consts)
            pool.do(lambda e: e.memset(ones[:, :], 1.0), consts)
            pool.do(lambda e: e.memset(taken[:, :], 0.0), consts)
            pool.do(lambda e: e.iota(expert_no[:, :], pattern=[[1, E]], base=0, channel_multiplier=0,
                                     allow_small_or_imprecise_dtypes=True), consts)
            m = pool.do(lambda e: e.iota(blank[:, :, 0], pattern=[[0, E]], base=N, channel_multiplier=1), consts)
            mark["consts"] = m
            for q in (pool, dve, pe, act):
                q.wait(m)
            mark["mask_cols"] = load(in_const, mask_cols_in[:, :], mask_cols)
            load(in_const, bias_row[:, :], gate_bias.broadcast_to([P, E]))
            m = (in_const, in_const.value)
            dve.wait(m)
            mark["value_scale"] = dve.do(lambda e: e.tensor_scalar(value_scale[:, :], mask_cols_in[:, :],
                                                                   V_S / (W_S * C_S), None, ALU.mult), dve_route)
            act.wait(mark["value_scale"])
            dve.wait(mark["value_scale"])

        def blank_rows():
            load(out_blank, slot_table.rearrange("(p e) c -> p (e c)", e=E), blank[:, :, :].rearrange("p e c -> p (e c)"),
                 mark["consts"])
            load(out_blank, xn2_rows[N:N + CAP, :], xn2[:, 0, :])
            load(out_blank, out[N:N + CAP, :], xn2[:, 0, :])
            mark["blank"] = (out_blank, out_blank.value)

        weight_jobs = []

        def weight_job(name, dst, src, rows, cols):
            weight_jobs.append((name, dst, src, rows, cols))

        def rows_of(w):
            return w.rearrange("(k p) n -> p k n", p=P)

        def plan_weights():
            weight_job("wk", wk_s, rows_of(wk), KC, KV * HD)
            weight_job(("wq", 0), wq_s[:, :, 0:512], rows_of(wq)[:, :, 0:512], KD, 512)
            weight_job("wv", wv_s, rows_of(wv), KC, KV * HD)
            for c in range(4):
                if c:
                    weight_job(("wq", c), wq_s[:, :, c * 512:(c + 1) * 512], rows_of(wq)[:, :, c * 512:(c + 1) * 512], KD, 512)
                weight_job(("wo", c), wo_s[:, 4 * c:4 * c + 4, :], rows_of(wo)[:, 4 * c:4 * c + 4, :], 4, D)
            weight_job("gate", gate_s, rows_of(gate_t), KD, E)
            weight_job("sg", sg_s, rows_of(shared_gate), KD, FS)
            weight_job("su", su_s, rows_of(shared_up), KD, FS)
            weight_job("sd", sd_s, rows_of(shared_down), FSB, D)

        loaded, prepared = [0], [0]

        def load_weight():
            if loaded[0] == len(weight_jobs):
                return
            n = loaded[0]
            name, dst, src, rows, cols = weight_jobs[n]
            buf = weight_in[n % 2][:, 0:rows * cols].rearrange("p (k n) -> p k n", k=rows)
            mark["in", name] = load(in_weight[n % 2], buf, src, mark.get(("weight_free", n % 2)))
            loaded[0] += 1

        def prepare_weight():
            n = prepared[0]
            name, dst, src, rows, cols = weight_jobs[n]
            buf = weight_in[n % 2][:, 0:rows * cols].rearrange("p (k n) -> p k n", k=rows)
            prepared[0] += 1
            for k in range(rows):
                mark[name] = mark["weight_free", n % 2] = split_sbuf(buf[:, k], dst[:, k], W_S, mark["in", name])
                if k < rows - 1:
                    yield
            load_weight()
            yield

        def load_x(b):
            mark["x", b] = load(in_x[b % 2], x_in[b % 2][:, :, :],
                                x[b * T:(b + 1) * T, :].rearrange("(t p) d -> p t d", p=P), mark.get(("x1", b - 2)))

        def load_ctx(b):
            mark["ctx_in", b] = load(in_ctx, ctx_in[:, :, :], ctx_t[:, b * S:(b + 1) * S].rearrange("(k p) s -> p k s", p=P),
                                     mark.get(("ctx", b - 1)))

        def prepare_ctx(b):
            mark["ctx", b] = split_sbuf(ctx_in[:, :, :], ctx_s[b % 2], C_S, mark["ctx_in", b],
                                        mark.get(("key_pe", (b - 1) * KV - 1)))

        def load_mask(b):
            mark["mask_in", b] = load(in_mask, mask_in[:, :], mask[b:b + 1, :].broadcast_to([P, S]),
                                      mark.get(("mask", b - 1)))

        def prepare_mask(b):
            pool.wait(mark["mask_in", b], mark.get(("max", (b - 1) * KV - 1)))
            mark["mask", b] = pool.do(lambda e: e.tensor_scalar(mask_add[b % 2][:, :], mask_in[:, :], -1.0, MASKED,
                                                                ALU.add, ALU.mult), pool_mask)

        def layer_norm(src, dst, ready, free):
            dve.wait(ready, mark.get("rstd"))
            for t in range(TB):
                m = dve.do(lambda e, t=t: e.bn_stats(stats[:, t, :], src[:, t, :]), dve_stats)
                if t < TB - 1:
                    yield
            dve.wait(m)
            for t in range(TB):
                m = dve.do(lambda e, t=t: e.bn_aggr(mean_var[:, t, :], stats[:, t, :]), dve_stats)
            pool.wait(m, mark.get("normed_last"))
            m = pool.do(lambda e: e.tensor_scalar(var_eps[:, :], mean_var[:, :, 1], LN_EPS, 1.0, ALU.add, ALU.mult), pool_rstd)
            pool.wait(m)
            m = mark["rstd"] = pool.do(lambda e: e.tensor_tensor(rstd[:, :], var_eps[:, :], minus_half[:, :], ALU.pow), pool_rstd)
            yield
            yield
            dve.wait(m, *free)
            for t in range(TB):
                mark["normed_last"] = dve.do(lambda e, t=t: e.tensor_scalar(
                    dst[:, t, :], src[:, t, :], mean_var[:, t, 0:1], rstd[:, t:t + 1], ALU.subtract, ALU.mult), dve_normed)

        def transpose_rows(src, dst, t, ready, free, scale):
            fill, ps = filler_bank()
            pe.wait(ready, bank_free.get(fill))
            for k in range(KD):
                m = pe.do(lambda e, k=k: e.transpose(ps[:, k * P:(k + 1) * P], src[:, t, k * P:(k + 1) * P], ident[:, :]),
                          pe_fill if k == KD - 1 else None)
            act.wait(*free)
            r = split_psum(ps[:, :].rearrange("p (k t) -> p k t", k=KD), dst[:, :, t * P:(t + 1) * P], scale, m)
            bank_free[fill] = r
            return r

        def query(i, h):
            b, g = divmod(i, KV)
            pe.wait(mark["xn_t", b], mark["wq", g // 2], bank_free.get("query"))
            n = (g * PAIR + h) * HD
            m = products(ps_query[:, h * T:(h + 1) * T],
                         [(wq_s[:, k, n:n + HD], xn_t[b % 2][:, k, :]) for k in range(KD)],
                         pe_query if h == PAIR - 1 else None)
            if h < PAIR - 1:
                return
            act.wait(mark.get(("score_pe", i - 1)))
            mark["query_pe", i] = m
            mark["query", i] = bank_free["query"] = split_psum(ps_query[:, :], q_t, 1.0 / (W_S * X_S), m)

        def key(i):
            b, g = divmod(i, KV)
            pe.wait(mark["ctx", b], mark["wk"], bank_free.get("fill0"))
            m = products(ps_fill[0][:, 0:S], [(wk_s[:, k, g * HD:(g + 1) * HD], ctx_s[b % 2][:, k, :]) for k in range(KC)], pe_key)
            mark["key_pe", i] = m
            act.wait(mark.get(("score_pe", i - 1)))
            mark["key", i] = bank_free["fill0"] = split_psum(ps_fill[0][:, 0:S], k_t, 1.0 / (W_S * C_S), m)

        def value(b, half, s):
            cols = slice(half * 512, (half + 1) * 512)
            fill, ps = filler_bank()
            pe.wait(mark["ctx", b], mark["wv"], bank_free.get(fill))
            m = products(ps[:, :], [(ctx_s[b % 2][:, k, s * P:(s + 1) * P], wv_s[:, k, cols]) for k in range(KC)], pe_fill)
            act.wait(mark.get(("head_pe", (b - 1) * KV - 1)))
            n = b * SB + s
            mark["value", b, half, s] = bank_free[fill] = split_psum(
                ps[:, :], v_s[b % 2][:, s, cols], None, m, vector_scale=value_scale[:, n:n + 1])

        def scores(i):
            pe.wait(mark["query", i], mark["key", i], bank_free.get("score"))
            for h in range(PAIR):
                for t in range(TB):
                    c = h * T + t * P
                    m = products(ps_score[h][:, t * S:(t + 1) * S], [(q_t[:, c:c + P], k_t)],
                                 pe_score if t == TB - 1 else None)
                mark["score_pe", i, h] = m
            mark["score_pe", i] = m

        def softmax_exp(i):
            b = i // KV
            dve.wait(mark["mask", b], mark.get(("low", i - 1)), mark.get(("norm", i - 1)))
            for c in range(PAIR * TB):
                h, t = divmod(c, TB)
                dve.wait(mark["score_pe", i, h])
                m = dve.do(lambda e, c=c, h=h, t=t: e.tensor_tensor_reduce(
                    out=probs[:, c, :], in0=ps_score[h][:, t * S:(t + 1) * S], in1=mask_add[b % 2][:, :],
                    scale=-SCORE_SCALE, scalar=3e38, op0=ALU.add, op1=ALU.min, accum_out=neg_max[:, c:c + 1]), dve_max)
                act.wait(m)
                a = act.do(lambda e, c=c: e.activation(probs[:, c, :], probs[:, c, :], ACT.Exp, bias=neg_max[:, c:c + 1],
                                                       scale=-1.0, accum_out=prob_sum[:, c:c + 1]), act_exp)
            mark["max", i] = bank_free["score"] = m
            mark["exp", i] = a

        def softmax_norm(i):
            dve.wait(mark["exp", i], mark.get(("norm", i - 1)))
            r = dve.do(lambda e: e.reciprocal(prob_inv[:, :], prob_sum[:, :]), dve_inv)
            dve.wait(r)
            r = dve.do(lambda e: e.tensor_scalar(prob_scale[:, :], prob_inv[:, :], P_S, None, ALU.mult), dve_inv)
            pool.wait(r, mark.get(("probs", i - 1)))
            for c in range(PAIR * TB):
                mark["norm", i, c] = pool.do(lambda e, c=c: e.tensor_scalar(
                    p_rows[:, 0, c, :], probs[:, c, :], prob_scale[:, c:c + 1], 1.0, ALU.mult, ALU.mult), pool_norm)
            mark["norm", i] = mark["norm", i, PAIR * TB - 1]
            dve.wait(r)

        def softmax_low(i, cs):
            for c in cs:
                dve.wait(mark["norm", i, c])
                mark["low", i] = dve.do(lambda e, c=c: e.scalar_tensor_tensor(
                    p_rows[:, 1, c, :], probs[:, c, :], prob_scale[:, c:c + 1], p_rows[:, 0, c, :], ALU.mult, ALU.subtract),
                    dve_low)

        def transpose_probs(i):
            sync.wait(mark["norm", i], mark["low", i], mark.get(("head_pe", i - 1)), mark.get(("probs", i - 1)))
            mark["probs", i] = sync.do(lambda e: e.dma_start_transpose(
                p_both[:, :, :, :, :].rearrange("p h c s t -> p (h c s) t"),
                p_rows[:, :, :, :].rearrange("p h c s -> p (h c s)")), turned, 16)

        def attend(i):
            b, g = divmod(i, KV)
            pe.wait(mark["probs", i], mark["value", b, g // 4, 0], mark["value", b, g // 4, 1], bank_free.get("head"))
            m = products(ps_head[:, :], [(v_s[b % 2][:, s, g * HD:(g + 1) * HD], p_t[s]) for s in range(SB)], pe_head)
            mark["head_pe", i] = m
            act.wait(mark.get(("out_pe", i - 1)))
            mark["head", i] = bank_free["head"] = split_psum(ps_head[:, :], o_t, 1.0 / P_S, m)

        def project(i):
            b, g = divmod(i, KV)
            pe.wait(mark["head", i], mark["wo", g // 2], bank_free.get("out") if g == 0 else None)
            for t in range(TB):
                m = products(ps_out[t][:, :], [(o_t[:, h * T + t * P:h * T + (t + 1) * P], wo_s[:, g * PAIR + h, :])
                                               for h in range(PAIR)],
                             pe_out if t == TB - 1 else None, first=g == 0, last=g == KV - 1)
            mark["out_pe", i] = m

        def residual(b):
            dve.wait(mark["out_pe", b * KV + KV - 1], mark["x", b], mark.get(("rows_out", b - 1)))
            for t in range(TB):
                m = dve.do(lambda e, t=t: e.scalar_tensor_tensor(x1[:, t, :], ps_out[t][:, :], 1.0 / (V_S * W_S),
                                                                 x_in[b % 2][:, t, :], ALU.mult, ALU.add), dve_residual)
                mark["x1", b] = bank_free["out"] = m
                yield

        def gate(b):
            fill, ps = filler_bank()
            pe.wait(mark["xn2_t", b], mark["gate"], bank_free.get(fill))
            for t in range(TB):
                m = products(ps[:, t * E:(t + 1) * E],
                             [(xn2_t[:, k, t * P:(t + 1) * P], gate_s[:, k, :]) for k in range(KD)],
                             pe_fill if t == TB - 1 else None)
            act.wait(m)
            m = act.do(lambda e: e.activation(exp_neg[:, :, :], ps[:, 0:TB * E].rearrange("p (t e) -> p t e", e=E),
                                              ACT.Exp, scale=-1.0 / (W_S * X_S)), act_fn)
            bank_free[fill] = mark["exp_neg", b] = m

        def chain(build_):
            m = dve.do(build_, dve_route)
            dve.wait(m)
            return m

        def choose(b):
            dve.wait(mark["exp_neg", b])
            chain(lambda e: e.tensor_scalar(exp_neg[:, :, :], exp_neg[:, :, :], 1.0, None, ALU.add))
            chain(lambda e: e.reciprocal(score[:, :, :], exp_neg[:, :, :]))
            mark["score_read", b] = chain(lambda e: e.tensor_tensor(
                biased[:, :, :], score[:, :, :], bias_row[:, :].unsqueeze(1).broadcast_to([P, TB, E]), ALU.add))
            yield
            flat = biased[:, :, :].rearrange("p t e -> p (t e)")
            for g in range(TB * GROUPS):
                m = dve.do(lambda e, g=g: e.max(group_top[:, g, :], flat[:, g * EPG:(g + 1) * EPG]), dve_route)
            dve.wait(m)
            yield
            top = group_top[:, :, :].rearrange("p (t g) k -> p t g k", t=TB)
            chain(lambda e: e.tensor_tensor(group_score[:, :, :], top[:, :, :, 0], top[:, :, :, 1], ALU.add))
            yield
            full = [P, TB, GROUPS, GROUPS]
            mine = group_score[:, :, :].unsqueeze(3).broadcast_to(full)
            other = group_score[:, :, :].unsqueeze(2).broadcast_to(full)
            dve.do(lambda e: e.tensor_tensor(beats[:, :, :, :], other, mine, ALU.is_gt))
            chain(lambda e: e.tensor_tensor(ties[:, :, :, :], other, mine, ALU.is_equal))
            chain(lambda e: e.tensor_tensor(ties[:, :, :, :], ties[:, :, :, :],
                                            lower[:, :, :].unsqueeze(1).broadcast_to(full), ALU.mult))
            chain(lambda e: e.tensor_tensor(beats[:, :, :, :], beats[:, :, :, :], ties[:, :, :, :], ALU.add))
            yield
            chain(lambda e: e.reduce_sum(group_rank[:, :, :], beats[:, :, :, :], AX.X))
            chain(lambda e: e.tensor_scalar(group_rank[:, :, :], group_rank[:, :, :], float(TOPG), None, ALU.is_lt))
            yield
            by_group = biased[:, :, :].rearrange("p t (g e) -> p (t g) e", g=GROUPS)
            chain(lambda e: e.tensor_tensor(by_group, by_group, group_rank[:, :, :].rearrange("p t g -> p (t g)")
                                            .unsqueeze(2).broadcast_to([P, TB * GROUPS, EPG]), ALU.mult))
            for t in range(TB):
                m = dve.do(lambda e, t=t: e.max(top8[:, t, :], biased[:, t, :]), dve_route)
            dve.wait(m)
            yield
            for t in range(TB):
                m = dve.do(lambda e, t=t: e.max_index(top8_at[:, t, :], top8[:, t, :], biased[:, t, :]), dve_route)
            dve.wait(m)
            yield
            chain(lambda e: e.tensor_copy(chosen[:, :, :], top8_at[:, :, 0:TOPK]))
            for t in range(TB):
                m = dve.do(lambda e, t=t: e.tensor_tensor(
                    one_hot[:, t, :, :], expert_no[:, :].unsqueeze(1).broadcast_to([P, TOPK, E]),
                    chosen[:, t, :].unsqueeze(2).broadcast_to([P, TOPK, E]), ALU.is_equal), dve_route)
            yield
            dve.wait(m, mark.get(("rank_pe", b - 1)))

            def count_uses(e):
                with nc.allow_low_precision(reason="0 and 1 are exact in float16"):
                    return e.reduce_sum(uses[:, :, :], one_hot[:, :, :, :].rearrange("p t k e -> p t e k"), AX.X)
            mark["uses", b] = dve.do(count_uses, dve_route)
            yield
            yield from pick(score, weight)
            yield
            chain(lambda e: e.reduce_sum(weight_sum[:, :], weight[:, :, :], AX.X))
            chain(lambda e: e.tensor_scalar(weight_sum[:, :], weight_sum[:, :], 1e-20, None, ALU.add))
            chain(lambda e: e.reciprocal(weight_inv[:, :], weight_sum[:, :]))
            chain(lambda e: e.tensor_scalar(weight_inv[:, :], weight_inv[:, :], ROUTE_SCALE, None, ALU.mult))
            yield
            dve.wait(mark.get(("scattered", b - 2)))
            mark["weight", b] = dve.do(lambda e: e.tensor_tensor(
                entry[b % 2][:, :, :, 1].bitcast(F32), weight[:, :, :], weight_inv[:, :].unsqueeze(2).broadcast_to([P, TB, TOPK]),
                ALU.mult), dve_route)
            yield

        def pick(table_, dst):
            for t in range(TB):
                m = dve.do(lambda e, t=t: e.tensor_tensor(
                    picked[:, t, :, :], one_hot[:, t, :, :], table_[:, t, :].unsqueeze(1).broadcast_to([P, TOPK, E]), ALU.mult),
                    dve_route)
            dve.wait(m)
            yield
            chain(lambda e: e.reduce_sum(dst[:, :, :], picked[:, :, :, :], AX.X))

        def rank(b):
            fill, ps = filler_bank()
            pe.wait(mark["uses", b], bank_free.get(fill))
            for t in range(TB):
                for u in range(t + 1):
                    pe.do(lambda e, t=t, u=u: e.matmul(ps[:, t * E:(t + 1) * E], (earlier if u == t else ones)[:, :],
                                                       uses[:, u, :], start=u == 0, stop=u == t))
            for u in range(TB):
                m = pe.do(lambda e, u=u: e.matmul(ps[:, TB * E:(TB + 1) * E], ones[:, :], uses[:, u, :], start=u == 0,
                                                  stop=u == TB - 1), pe_fill if u == TB - 1 else None)
            mark["rank_pe", b] = m

        def place(b):
            fill, ps = filler_bank()
            dve.wait(mark["rank_pe", b])
            chain(lambda e: e.tensor_tensor(position[:, :, :], ps[:, 0:TB * E].rearrange("p (t e) -> p t e", e=E),
                                            taken[:, :].unsqueeze(1).broadcast_to([P, TB, E]), ALU.add))
            bank_free[fill] = chain(lambda e: e.tensor_tensor(taken[:, :], ps[:, TB * E:(TB + 1) * E], taken[:, :], ALU.add))

        def find_slots(b):
            yield from pick(position, my_position)
            chain(lambda e: e.scalar_tensor_tensor(slot_f[:, :, :], my_position[:, :, :], float(E), chosen[:, :, :],
                                                   ALU.mult, ALU.add))
            mark["slot", b] = dve.do(lambda e: e.tensor_copy(slot_at[b % 2][:, :, :], slot_f[:, :, :]), dve_route)
            yield

        def record(b):
            pool.wait(mark.get(("scattered", b - 2)))
            pool.do(lambda e: e.iota(entry[b % 2][:, :, :, 0], pattern=[[P, TB], [0, TOPK]], base=b * T, channel_multiplier=1),
                    pool_entry)
            pool.wait((pool_entry, pool_entry.value), mark["weight", b], mark["slot", b], mark["blank"])
            for t in range(TB):
                for k in range(TOPK):
                    m = pool.do(lambda e, t=t, k=k: e.indirect_dma_start(
                        slot_table, bass.IndirectOffsetOnAxis(ap=slot_at[b % 2][:, t, k:k + 1], axis=0),
                        entry[b % 2][:, t, k, :], None, bounds_check=CAP * E - 1, oob_is_err=False), scattered[b % 2], 16)
            mark["scattered", b] = m

        def swiglu(g_psum, u_psum, dst, scale, ready, free):
            k = 1.0 / (W_S * X_S)
            act.wait(ready, mark.get("glu_last"))
            m = act.do(lambda e: e.activation(tanh_g[:, :], g_psum, ACT.Tanh, scale=0.5 * k), act_fn)
            dve.wait(m)
            m = dve.do(lambda e: e.scalar_tensor_tensor(gated[:, :], tanh_g[:, :], 1.0, g_psum, ALU.add, ALU.mult), dve_glu)
            dve.wait(m, *free)
            m = dve.do(lambda e: e.scalar_tensor_tensor(dst, gated[:, :], 0.5 * k * k * scale, u_psum, ALU.mult, ALU.mult), dve_glu)
            mark["glu_last"] = m
            return m

        def shared_up_part(b, f):
            fill, ps = filler_bank()
            pe.wait(mark["xn2_t", b], mark["sg"], mark["su"], bank_free.get(fill))
            for n, w in enumerate((sg_s, su_s)):
                m = products(ps[:, n * T:(n + 1) * T], [(w[:, k, f * P:(f + 1) * P], xn2_t[:, k, :]) for k in range(KD)],
                             pe_fill if n else None)
            mark["xn2_t_read", b] = m
            m = swiglu(ps[:, 0:T], ps[:, T:2 * T], hidden[:, :], HS_S, m, [mark.get("hidden_read")])
            bank_free[fill] = m
            pool.wait(m, mark.get(("shared_pe", b - 1)))
            m = pool.do(lambda e: e.tensor_scalar(h_t.hi[:, f, :], hidden[:, :], 1.0, 1.0, ALU.mult, ALU.mult), pool_hi)
            pool.wait(m)
            mark["hidden", b] = mark["hidden_read"] = pool.do(
                lambda e: e.tensor_tensor(h_t.lo[:, f, :], hidden[:, :], h_t.hi[:, f, :], ALU.subtract), pool_hi)

        def shared_down_part(b, t):
            fill, ps = filler_bank()
            pe.wait(mark["hidden", b], mark["sd"], bank_free.get(fill))
            m = products(ps[:, :], [(h_t[:, f, t * P:(t + 1) * P], sd_s[:, f, :]) for f in range(FSB)], pe_fill)
            mark["shared_pe", b] = m
            dve.wait(m, mark["x1", b])
            m = bank_free[fill] = dve.do(lambda e: e.scalar_tensor_tensor(
                x1[:, t, :], ps[:, :], 1.0 / (HS_S * W_S), x1[:, t, :], ALU.mult, ALU.add), dve_residual)
            r = b * T + t * P
            mark["rows_out", b] = load(out_rows, out[r:r + P, :], x1[:, t, :], m)

        def normalise_x(b):
            yield from layer_norm(x_in[b % 2], normed, mark["x", b], [mark.get(("xn_t", b - 1))])
            mark["normed", b] = mark["normed_last"]
            yield

        def x_t(b, t):
            mark["xn_t", b] = transpose_rows(normed, xn_t[b % 2], t, mark["normed", b],
                                             [mark.get(("query_pe", (b - 1) * KV - 1))], X_S)

        def normalise_x1(b):
            yield from layer_norm(x1, xn2, mark["x1", b],
                                  [mark.get(("xn2_out", b - 1)), mark.get(("xn2_t", b - 1)), mark["blank"]])
            m = mark["xn2", b] = mark["normed_last"]
            mark["xn2_out", b] = load(out_xn2, xn2_rows[b * T:(b + 1) * T, :].rearrange("(t p) d -> p t d", p=P),
                                      xn2[:, :, :], m)
            yield

        def xn2_transposed(b, t):
            mark["xn2_t", b] = transpose_rows(xn2, xn2_t, t, mark["xn2", b], [mark.get(("xn2_t_read", b - 1))], X_S)

        def fillers(b, j):
            ahead, behind = b + 1 < B, 0 <= b - 1
            a, z = b + 1, b - 1
            none = lambda: None
            table_ = {
                0: [ahead and (lambda: value(a, 0, 0)), ahead and (lambda: value(a, 0, 1))],
                1: [ahead and (lambda: value(a, 1, 0)), ahead and (lambda: value(a, 1, 1))],
                2: [behind and (lambda: xn2_transposed(z, 0)), behind and (lambda: xn2_transposed(z, 1))],
                3: [behind and (lambda: gate(z)), behind and (lambda: shared_up_part(z, 0))],
                4: [ahead and (lambda: x_t(a, 0)), behind and (lambda: shared_up_part(z, 1))],
                5: [ahead and (lambda: x_t(a, 1)), behind and (lambda: shared_up_part(z, 2))],
                6: [behind and (lambda: (rank(z), place(z))), behind and (lambda: shared_up_part(z, 3))],
                7: [behind and (lambda: shared_down_part(z, 0)), behind and (lambda: shared_down_part(z, 1))],
            }
            return [f or none for f in table_[j]]

        def begin_side_work(b, j):
            ahead, behind = b + 1 < B, 0 <= b - 1
            if j == 1:
                finish("residual")
                if behind:
                    begin("x1 normed", normalise_x1(b - 1))
                if ahead:
                    load_x(b + 1)
                    load_mask(b + 1)
            if j == 2 and ahead:
                prepare_mask(b + 1)
                begin("x normed", normalise_x(b + 1))
            if j == 4 and b + 2 < B:
                load_ctx(b + 2)

        before_fillers = {2: "x1 normed", 4: "x normed", 6: "chosen"}

        def prologue():
            plan_weights()
            load_ctx(0)
            load_weight()
            load_x(0)
            load_weight()
            load_mask(0)
            constants()
            blank_rows()
            prepare_ctx(0)
            load_ctx(1)
            begin("wk", prepare_weight())
            begin("x", normalise_x(0))
            finish("x")
            for t in range(TB):
                x_t(0, t)
            key(0)
            begin("wq", prepare_weight())
            finish("wq")
            for h in range(PAIR):
                query(0, h)
            prepare_mask(0)
            prepare_ctx(1)

        prepare_at = {0: 2, 2: 2, 4: 2, 6: 2, 7: 1, 8: 1, 9: 1}

        def attention():
            for i in range(TURNS + 1):
                b, j = divmod(i, KV)
                for _ in range(prepare_at.get(i, 0) + (i == 0)):
                    begin("weight", prepare_weight())
                    if i == 0 and "wv" not in mark:
                        finish("weight")
                if i < TURNS:
                    begin_side_work(b, j)
                    scores(i)
                    softmax_exp(i)
                if i == 0:
                    for half in range(2):
                        for s in range(SB):
                            value(0, half, s)
                if i + 1 < TURNS:
                    key(i + 1)
                    query(i + 1, 0)
                piece()
                if i < TURNS:
                    softmax_norm(i)
                if j in before_fillers:
                    finish(before_fillers[j])
                first, second = fillers(b, j) if i < TURNS else (lambda: None,) * 2
                use[0] = 1
                first()
                if i < TURNS and b and j == 3:
                    begin("chosen", choose(b - 1))
                if i < TURNS and b and j == 6:
                    begin("slots", find_slots(b - 1))
                piece()
                if i < TURNS:
                    softmax_low(i, range(0, PAIR * TB // 2))
                if i:
                    attend(i - 1)
                if i < TURNS:
                    softmax_low(i, range(PAIR * TB // 2, PAIR * TB))
                    transpose_probs(i)
                piece()
                if i + 1 < TURNS:
                    query(i + 1, 1)
                piece()
                use[0] = 0
                second()
                piece()
                if i:
                    project(i - 1)
                piece()
                if prepare_at.get(i, 0):
                    finish("weight")
                if i < TURNS and j == 7:
                    if b:
                        finish("slots")
                        record(b - 1)
                    if b + 2 < B:
                        prepare_ctx(b + 2)
                if i and j == 0:
                    begin("residual", residual(b - 1))
                piece()

        def expert_views(n):
            w = expert_in[n % AHEAD]
            up = w[:, 0:KD * 2 * F].rearrange("p (k n) -> p k n", k=KD)
            down = w[:, KD * 2 * F:].rearrange("p (k n) -> p k n", k=FB)
            return up, down

        def load_expert(e_):
            up, down = expert_views(e_)
            after = [mark.get(("expert_split", e_ - AHEAD)), mark["query_pe", TURNS - 1], mark["key_pe", TURNS - 1]]
            sig = in_expert[e_ % AHEAD]
            load(sig, up[:, :, 0:F], w1[e_].rearrange("(p k) n -> p k n", p=P), *after)
            load(sig, up[:, :, F:2 * F], w3[e_].rearrange("(p k) n -> p k n", p=P))
            mark["expert_in", e_] = load(sig, down, w2[e_].rearrange("(p k) n -> p k n", p=P))

        def prepare_expert(e_, part):
            src, dst = expert_in[e_ % AHEAD], expert_w[e_ % AHEAD]
            third = EW // 3
            at = slice(part * third, (part + 1) * third)
            free = [mark.get(("expert_y_pe", e_ - AHEAD)), mark["out_pe", TURNS - 1]]
            if part < 2:
                act.wait(mark["expert_in", e_], *free)
                m = act.do(lambda e: e.activation(dst.hi[:, at], src[:, at], ACT.Copy, scale=W_S), act_hi)
            else:
                pool.wait(mark["expert_in", e_], *free)
                m = pool.do(lambda e: e.tensor_scalar(dst.hi[:, at], src[:, at], W_S, 1.0, ALU.mult, ALU.mult), pool_hi)
            dve.wait(mark["expert_in", e_], m, *free)
            mark["expert_split", e_] = dve.do(lambda e: e.scalar_tensor_tensor(
                dst.lo[:, at], src[:, at], W_S, dst.hi[:, at], ALU.mult, ALU.subtract), dve_lo)

        def load_table():
            m = load(in_table, table[:, :, :].rearrange("p e c -> p (e c)"), slot_table.rearrange("(p e) c -> p (e c)", e=E),
                     mark["scattered", B - 1], mark["scattered", B - 2])
            dve.wait(m)
            pool.wait(m)
            mark["slot_weight"] = dve.do(lambda e: e.tensor_scalar(slot_weight[:, :], table[:, :, 1].bitcast(F32),
                                                                   1.0 / (HE_S * W_S), None, ALU.mult), dve_route)
            act.wait(mark["slot_weight"])

        def gather(e_):
            pool.wait(mark.get(("rows_pe", e_ - 3)), mark["xn2_out", B - 1], mark["x1", B - 1], mark["x1", B - 2])
            mark["gathered", e_] = pool.do(lambda e: e.indirect_dma_start(
                rows_in[e_ % 3], None, xn2_rows, bass.IndirectOffsetOnAxis(ap=table[:, e_, 0:1], axis=0),
                bounds_check=N + CAP - 1, oob_is_err=True), gathered[e_ % 3], 16)

        def expert_rows(e_):
            rows = rows_in[e_ % 3].rearrange("c (p k) -> c k p", k=KD)
            ps = ps_fill[e_ % 2]
            pe.wait(mark["gathered", e_], bank_free.get(f"fill{e_ % 2}"))
            for k in range(KD):
                m = pe.do(lambda e, k=k: e.transpose(ps[:, k * P:(k + 1) * P], rows[:, k, :], ident[:, :]),
                          pe_fill if k == KD - 1 else None)
            mark["rows_pe", e_] = m
            act.wait(mark.get(("expert_up_pe", e_ - 2)), mark["query_pe", TURNS - 1])
            mark["rows_t", e_] = bank_free[f"fill{e_ % 2}"] = split_psum(
                ps[:, :].rearrange("p (k c) -> p k c", k=KD), rows_t[e_ % 2][:, :, 0:P], X_S, m)

        def expert_up(e_):
            ps = ps_score[e_ % 2]
            w = expert_w[e_ % AHEAD][:, 0:KD * 2 * F]
            pe.wait(mark["rows_t", e_], mark["expert_split", e_], bank_free.get(f"up{e_ % 2}"), bank_free.get("score"))
            m = products(ps[:, :], [(rows_t[e_ % 2][:, k, 0:P], w[:, k * 2 * F:(k + 1) * 2 * F]) for k in range(KD)], pe_score)
            mark["expert_up_pe", e_] = m
            mark["expert_h", e_] = bank_free[f"up{e_ % 2}"] = swiglu(
                ps[:, 0:F], ps[:, F:2 * F], expert_h, HE_S, m, [mark.get(("expert_ht_pe", e_ - 1)), mark["xn_t", B - 1]])

        def expert_hidden(e_):
            cols = expert_h.rearrange("c (p f) -> c f p", f=FB)
            ps = (ps_head, ps_query)[e_ % 2]
            pe.wait(mark["expert_h", e_], bank_free.get(("head", "query")[e_ % 2]))
            for f in range(FB):
                m = pe.do(lambda e, f=f: e.transpose(ps[:, f * P:(f + 1) * P], cols[:, f, :], ident[:, :]),
                          pe_trans if f == FB - 1 else None)
            mark["expert_ht_pe", e_] = m
            act.wait(mark.get(("expert_y_pe", e_ - 2)), mark[("shared_pe", B - 1)])
            mark["expert_ht", e_] = bank_free[("head", "query")[e_ % 2]] = split_psum(
                ps[:, 0:FB * P].rearrange("p (f c) -> p f c", f=FB), expert_h_t[e_ % 2], 1.0, m)

        def expert_down(e_):
            ps = ps_out[e_ % 2]
            w = expert_w[e_ % AHEAD][:, KD * 2 * F:]
            pe.wait(mark["expert_ht", e_], bank_free.get(f"y{e_ % 2}"), bank_free.get("out"))
            m = products(ps[:, :], [(expert_h_t[e_ % 2][:, f, :], w[:, f * D:(f + 1) * D]) for f in range(FB)], pe_out)
            mark["expert_y_pe", e_] = m
            act.wait(m, mark.get(("added", e_ - 4)), mark["sd"])
            m = bank_free[f"y{e_ % 2}"] = act.do(lambda e: e.activation(
                expert_y[e_ % 4], ps[:, :], ACT.Copy, scale=slot_weight[:, e_:e_ + 1]), act_y)
            pool.wait(m, mark.get(("added", e_ - 1)), mark["rows_out", B - 1])
            mark["added", e_] = pool.do(lambda e: e.indirect_dma_start(
                out, bass.IndirectOffsetOnAxis(ap=table[:, e_, 0:1], axis=0), expert_y[e_ % 4], None,
                bounds_check=N + CAP - 1, oob_is_err=True, compute_op=ALU.add), added, 16)

        def tail():
            z = B - 1
            for e_ in range(AHEAD):
                load_expert(e_)
            finish("residual")
            begin("x1 normed", normalise_x1(z))
            finish("x1 normed")
            for t in range(TB):
                use[0] = 1 - t
                xn2_transposed(z, t)
            gate(z)
            begin("chosen", choose(z))
            finish("chosen")
            shared_up_part(z, 0)
            rank(z)
            place(z)
            begin("slots", find_slots(z))
            finish("slots")
            record(z)
            load_table()
            for e_ in range(3):
                gather(e_)
            for f in range(1, FSB):
                use[0] = f % 2
                shared_up_part(z, f)
            for e_ in range(2):
                for part in range(3):
                    prepare_expert(e_, part)
                load_expert(e_ + AHEAD)
            for t in range(TB):
                shared_down_part(z, t)

        def experts():
            for e_ in range(2):
                expert_rows(e_)
                gather(e_ + 3)
            for e_ in range(E + 1):
                if e_ < E:
                    expert_up(e_)
                if e_ >= 1:
                    expert_down(e_ - 1)
                if e_ + 2 < E:
                    prepare_expert(e_ + 2, 0)
                if e_ < E:
                    expert_hidden(e_)
                if e_ + 2 < E:
                    prepare_expert(e_ + 2, 1)
                    prepare_expert(e_ + 2, 2)
                    expert_rows(e_ + 2)
                    if e_ + 5 < E:
                        gather(e_ + 5)
                    if e_ + 2 + AHEAD < E:
                        load_expert(e_ + 2 + AHEAD)
            pool.wait(mark["added", E - 1])
            sync.wait(mark["rows_out", B - 1], mark["xn2_out", B - 1], mark["blank"])

        prologue()
        attention()
        tail()
        experts()

        block = stack.enter_context(nc.Block())
        block.sync(sync.run)
        block.gpsimd(pool.run)
        block.scalar(act.run)
        block.vector(dve.run)
        block.tensor(pe.run)


def kernel(x, ctx_1024, mask_BxS2_bf1, L0_xattn_Wq, L0_xattn_Wk, L0_xattn_Wv, L0_xattn_Wo, L0_ffn_gate_w, L0_ffn_gate_bias,
           L0_ffn_w1, L0_ffn_w2, L0_ffn_w3, L0_ffn_shared_gate, L0_ffn_shared_up, L0_ffn_shared_down):
    import concourse.bacc as bacc
    from concourse.bass_utils import run_bass_kernel_spmd

    mask = np.ascontiguousarray(mask_BxS2_bf1).view(np.uint8)
    arrays = {
        "x": np.asarray(x).reshape(N, D),
        "ctx_t": np.asarray(ctx_1024).reshape(B * S, DC).T,
        "mask": mask,
        "mask_cols": mask.reshape(B * SB, P).T,
        "wq": L0_xattn_Wq, "wk": L0_xattn_Wk, "wv": L0_xattn_Wv, "wo": L0_xattn_Wo,
        "gate_t": np.asarray(L0_ffn_gate_w).T,
        "gate_bias": np.asarray(L0_ffn_gate_bias).reshape(1, E),
        "w1": L0_ffn_w1, "w2": L0_ffn_w2, "w3": L0_ffn_w3,
        "shared_gate": L0_ffn_shared_gate, "shared_up": L0_ffn_shared_up, "shared_down": L0_ffn_shared_down,
    }
    arrays = {k: np.ascontiguousarray(a) for k, a in arrays.items()}
    nc = bacc.Bacc("TRN2", target_bir_lowering=False, num_devices=1)
    args = [nc.dram_tensor(k, a.shape, mybir.dt.from_np(a.dtype), kind="ExternalInput").ap() for k, a in arrays.items()]
    out = nc.dram_tensor("out_rows_dram", (N + CAP, D), F32, kind="ExternalOutput").ap()
    build(nc, *args, out)
    got = run_bass_kernel_spmd(nc, [arrays], core_ids=[0])
    return got.results[0]["out_rows_dram"][:N].reshape(B, T, D)
```

```python
from collections import deque
from contextlib import ExitStack

import numpy as np

import concourse.bass as bass
import concourse.mybir as mybir

F32, F16, U32, U8 = mybir.dt.float32, mybir.dt.float16, mybir.dt.uint32, mybir.dt.uint8
ALU = mybir.AluOpType
ACT = mybir.ActivationFunctionType
AX = mybir.AxisListType

P = 128
B, T, D = 16, 256, 512
S, DC = 256, 256
HEADS, KV, HD = 16, 8, 128
PAIR = HEADS // KV
E, TOPK, GROUPS, TOPG = 32, 4, 4, 2
F, FS = 256, 512
ROUTE_SCALE = 2.0
CAP = 2 * (2 * 256 * TOPK // E)
N = B * T
EPG = E // GROUPS

TB, SB, KD, KC, FB, FSB = T // P, S // P, D // P, DC // P, F // P, FS // P
TURNS = B * KV
assert CAP == P

W_S = 64.0
X_S = 64.0
C_S = 16.0
V_S = 16.0
P_S = 1024.0
HS_S = 64.0
HE_S = 16.0
MASKED = 1e30
LN_EPS = 1e-5
SCORE_SCALE = 1.0 / float(np.sqrt(np.float32(HD)))


class Signal:

    def __init__(self, handle):
        self.handle, self.value = handle, 0


class Queue:

    def __init__(self):
        self.steps, self.seen = [], {}

    def wait(self, *marks):
        for mark in marks:
            if mark is None:
                continue
            signal, value = mark
            if self.seen.get(id(signal), 0) < value:
                self.seen[id(signal)] = value
                self.steps.append(lambda eng, h=signal.handle, v=value: eng.wait_ge(h, v))

    def do(self, build, signal=None, by=1):
        if signal is None:
            self.steps.append(build)
            return None
        self.steps.append(lambda eng, h=signal.handle: build(eng).then_inc(h, by))
        signal.value += by
        return (signal, signal.value)

    def run(self, eng):
        for step in self.steps:
            step(eng)


class Split:

    def __init__(self, hi, lo):
        self.hi, self.lo = hi, lo

    def __getitem__(self, at):
        return Split(self.hi[at], self.lo[at])


def build(nc, x, ctx_t, mask, mask_cols, wq, wk, wv, wo, gate_t, gate_bias, w1, w2, w3,
          shared_gate, shared_up, shared_down, out):
    stack = ExitStack()
    with stack:
        def sbuf(name, shape, dt=F32):
            return stack.enter_context(nc.sbuf_tensor(name, [P] + list(shape), dt))

        def split(name, shape):
            both = sbuf(name, [2] + list(shape), F16)
            if len(shape) == 1:
                return Split(both[:, 0, :], both[:, 1, :])
            return Split(both[:, 0], both[:, 1])

        def signal(name):
            return Signal(stack.enter_context(nc.semaphore(name)))

        xn2_rows = nc.dram_tensor("xn2_rows", (N + CAP, D), F32, kind="Internal").ap()
        slot_table = nc.dram_tensor("slot_table", (CAP * E, 2), U32, kind="Internal").ap()

        sizes = [(KC, KV * HD), (KC, KV * HD), (KD, HEADS * HD), (HEADS, D), (SB, KV * HD), (SB, KV * HD),
                 (PAIR * TB, S), (PAIR * TB, S), (PAIR * TB, S)]
        arena = sbuf("arena", [sum(2 * k * n for k, n in sizes)], F16)

        def carve():
            at = 0
            for k, n in sizes[:-3]:
                yield Split(*(arena[:, at + i * k * n:at + (i + 1) * k * n].rearrange("p (k n) -> p k n", k=k)
                              for i in (0, 1)))
                at += 2 * k * n
            for k, n in sizes[-3:]:
                yield arena[:, at:at + 2 * k * n]
                at += 2 * k * n
        wv_s, wk_s, wq_s, wo_s, v_s0, v_s1, probs_at, p_rows_at, p_both_at = carve()
        v_s = [v_s0, v_s1]
        sg_s = split("sg_s", [KD, FS])
        su_s = split("su_s", [KD, FS])
        sd_s = split("sd_s", [FSB, D])
        gate_s = split("gate_s", [KD, E])
        CHUNK = 2048
        weight_in = [sbuf(f"weight_in{n}", [CHUNK]) for n in range(2)]

        x_in = [sbuf(f"x_in{n}", [TB, D]) for n in range(2)]
        normed = sbuf("normed", [TB, D])
        xn_t = [split(f"xn_t{n}", [KD, T]) for n in range(2)]
        ctx_in = sbuf("ctx_in", [KC, S])
        ctx_s = [split(f"ctx_s{n}", [KC, S]) for n in range(2)]
        mask_in = sbuf("mask_in", [S], U8)
        mask_add = [sbuf(f"mask_add{n}", [S]) for n in range(2)]
        mask_cols_in = sbuf("mask_cols_in", [B * SB], U8)
        value_scale = sbuf("value_scale", [B * SB])
        q_t = split("q_t", [PAIR * T])
        k_t = split("k_t", [S])
        probs = probs_at.bitcast(F32).rearrange("p (c s) -> p c s", c=PAIR * TB)
        neg_max = sbuf("neg_max", [PAIR * TB])
        prob_sum = sbuf("prob_sum", [PAIR * TB])
        prob_inv = sbuf("prob_inv", [PAIR * TB])
        prob_scale = sbuf("prob_scale", [PAIR * TB])
        p_rows = p_rows_at.rearrange("p (h c s) -> p h c s", h=2, c=PAIR * TB)
        p_both = p_both_at.rearrange("p (h c s t) -> p h c s t", h=2, c=PAIR * TB, s=SB)
        p_t = [Split(p_both[:, 0, :, s, :], p_both[:, 1, :, s, :]) for s in range(SB)]
        o_t = split("o_t", [PAIR * T])
        stats = sbuf("stats", [TB, 6])
        mean_var = sbuf("mean_var", [TB, 2])
        var_eps = sbuf("var_eps", [TB])
        rstd = sbuf("rstd", [TB])
        minus_half = sbuf("minus_half", [TB])
        x1 = sbuf("x1", [TB, D])
        xn2 = sbuf("xn2", [TB, D])
        xn2_t = split("xn2_t", [KD, T])
        tanh_g = sbuf("tanh_g", [T])
        gated = sbuf("gated", [T])
        hidden = sbuf("hidden", [T])
        h_t = split("h_t", [FSB, T])
        bias_row = sbuf("bias_row", [E])
        exp_neg = sbuf("exp_neg", [TB, E])
        score = sbuf("score", [TB, E])
        biased = sbuf("biased", [TB, E])
        group_top = sbuf("group_top", [TB * GROUPS, 8])
        group_score = sbuf("group_score", [TB, GROUPS])
        beats = sbuf("beats", [TB, GROUPS, GROUPS])
        ties = sbuf("ties", [TB, GROUPS, GROUPS])
        lower = sbuf("lower", [GROUPS, GROUPS])
        group_rank = sbuf("group_rank", [TB, GROUPS])
        top8 = sbuf("top8", [TB, 8])
        top8_at = sbuf("top8_at", [TB, 8], U32)
        chosen = sbuf("chosen", [TB, TOPK])
        expert_no = sbuf("expert_no", [E])
        one_hot = sbuf("one_hot", [TB, TOPK, E])
        picked = sbuf("picked", [TB, TOPK, E])
        weight = sbuf("weight", [TB, TOPK])
        weight_sum = sbuf("weight_sum", [TB])
        weight_inv = sbuf("weight_inv", [TB])
        uses = sbuf("uses", [TB, E], F16)
        earlier = sbuf("earlier", [P], F16)
        ones = sbuf("ones", [P], F16)
        taken = sbuf("taken", [E])
        position = sbuf("position", [TB, E])
        my_position = sbuf("my_position", [TB, TOPK])
        slot_f = sbuf("slot_f", [TB, TOPK])
        slot_at = [sbuf(f"slot_at{n}", [TB, TOPK], U32) for n in range(2)]
        entry = [sbuf(f"entry{n}", [TB, TOPK, 2], U32) for n in range(2)]
        ident = sbuf("ident", [P])
        blank = sbuf("blank", [E, 2], U32)

        EW = KD * 2 * F + FB * D
        AHEAD = 6
        HELD = 3
        expert_in = [arena[:, 2 * n * EW:2 * (n + 1) * EW].bitcast(F32) for n in range(AHEAD)]
        expert_w = [Split(arena[:, 2 * n * EW:(2 * n + 1) * EW], arena[:, (2 * n + 1) * EW:(2 * n + 2) * EW])
                    for n in range(AHEAD, AHEAD + HELD)]
        rows_in = [x_in[0][:, 0, :], x_in[0][:, 1, :], x_in[1][:, 0, :]]
        rows_t = xn_t
        table = sbuf("table", [E, 2], U32)
        slot_weight = sbuf("slot_weight", [E])
        expert_h = normed[:, 0, 0:F]
        expert_h_t = [h_t[:, 0:FB, 0:P], h_t[:, FB:2 * FB, 0:P]]
        expert_y = [weight_in[n // 2][:, (n % 2) * D:(n % 2 + 1) * D] for n in range(4)]

        def bank(name):
            return stack.enter_context(nc.psum_tensor(name, [P, 512], F32))

        ps_score = [bank("ps_score0"), bank("ps_score1")]
        ps_fill = [bank("ps_fill0"), bank("ps_fill1")]
        ps_head = bank("ps_head")
        ps_query = bank("ps_query")
        ps_out = [bank("ps_out0"), bank("ps_out1")]
        bank_free = {}

        use = [1]

        def filler_bank():
            return f"fill{use[0]}", (ps_fill + ps_score)[use[0]]

        sync, pool, act, dve, pe = (Queue() for _ in range(5))

        consts = signal("consts")
        pe_query, pe_key, pe_score, pe_trans = (signal(n) for n in ("pe_query", "pe_key", "pe_score", "pe_trans"))
        pe_head, pe_out, pe_fill = signal("pe_head"), signal("pe_out"), signal("pe_fill")
        act_hi, dve_lo = signal("act_hi"), signal("dve_lo")
        pool_hi = signal("pool_hi")
        dve_max, act_exp, dve_inv, pool_norm = (signal(n) for n in ("dve_max", "act_exp", "dve_inv", "pool_norm"))
        dve_stats, pool_rstd, dve_normed = signal("dve_stats"), signal("pool_rstd"), signal("dve_normed")
        dve_residual, act_fn, dve_glu = signal("dve_residual"), signal("act_fn"), signal("dve_glu")
        dve_route, pool_entry, pool_mask = signal("dve_route"), signal("pool_entry"), signal("pool_mask")
        act_y = signal("act_y")
        in_weight = [signal(f"in_weight{n}") for n in range(2)]
        in_x = [signal(f"in_x{n}") for n in range(2)]
        in_ctx, in_mask, in_const = signal("in_ctx"), signal("in_mask"), signal("in_const")
        out_rows, out_xn2 = signal("out_rows"), signal("out_xn2")
        in_table = signal("in_table")
        scattered = [signal(f"scattered{n}") for n in range(2)]
        gathered = [signal(f"gathered{n}") for n in range(3)]
        in_expert = [signal(f"in_expert{n}") for n in range(AHEAD)]
        added = signal("added")
        dve_low, turned = signal("dve_low"), signal("turned")
        out_blank = signal("out_blank")

        mark = {}

        def load(signal_, dst, src, *after):
            sync.wait(*after)
            return sync.do(lambda e: e.dma_start(dst, src), signal_, 16)

        def product(dst, a, b, first, last):
            pe.do(lambda e: e.matmul(dst, a.hi, b.hi, start=first, stop=False))
            pe.do(lambda e: e.matmul(dst, a.hi, b.lo, start=False, stop=False))
            final = lambda e: e.matmul(dst, a.lo, b.hi, start=False, stop=last)
            return final

        def products(dst, pairs, sig=None, first=True, last=True):
            for n, (a, b) in enumerate(pairs):
                final = product(dst, a, b, first and n == 0, last and n == len(pairs) - 1)
                end = n == len(pairs) - 1
                m = pe.do(final, sig if end else None)
            return m

        def split_psum(src, dst, scale, ready, vector_scale=None):
            s = scale if vector_scale is None else vector_scale
            act.wait(ready)
            hi = act.do(lambda e: e.activation(dst.hi, src, ACT.Copy, scale=s), act_hi)
            dve.wait(hi)
            return dve.do(lambda e: e.scalar_tensor_tensor(dst.lo, src, s, dst.hi, ALU.mult, ALU.subtract), dve_lo)

        def split_sbuf(src, dst, scale, ready, free=None, on_act=False):
            if on_act:
                act.wait(ready, free)
                hi = act.do(lambda e: e.activation(dst.hi, src, ACT.Copy, scale=scale), act_hi)
            else:
                pool.wait(ready, free)
                hi = pool.do(lambda e: e.tensor_scalar(dst.hi, src, scale, 1.0, ALU.mult, ALU.mult), pool_hi)
            dve.wait(ready, free, hi)
            return dve.do(lambda e: e.scalar_tensor_tensor(dst.lo, src, scale, dst.hi, ALU.mult, ALU.subtract), dve_lo)

        side = deque()

        def begin(name, pieces):
            side.append((name, pieces))

        def piece():
            if side and next(side[0][1], "end") == "end":
                side.popleft()
                piece()

        def finish(name):
            while any(n == name for n, _ in side):
                _, pieces = side.popleft()
                for _ in pieces:
                    pass

        def constants():
            pool.do(lambda e: e.memset(ident[:, :], 0.0), consts)
            pool.do(lambda e: e.memset(earlier[:, :], 1.0), consts)
            pool.do(lambda e: e.memset(lower[:, :, :], 1.0), consts)
            pool.do(lambda e: e.memset(xn2[:, 0, :], 0.0), consts)
            pool.do(lambda e: e.memset(blank[:, :, 1], 0), consts)
            m = pool.do(lambda e: e.memset(minus_half[:, :], -0.5), consts)
            pool.wait(m)
            pool.do(lambda e: e.affine_select(out=ident[:, :], in_=ident[:, :], compare_op=ALU.not_equal, fill=1.0,
                                              base=0, pattern=[[-1, P]], channel_multiplier=1), consts)
            pool.do(lambda e: e.affine_select(out=earlier[:, :], in_=earlier[:, :], compare_op=ALU.is_gt, fill=0.0,
                                              base=0, pattern=[[1, P]], channel_multiplier=-1), consts)
            pool.do(lambda e: e.affine_select(out=lower[:, :, :], in_=lower[:, :, :], compare_op=ALU.is_gt, fill=0.0,
                                              base=0, pattern=[[1, GROUPS], [-1, GROUPS]], channel_multiplier=0), consts)
            pool.do(lambda e: e.memset(ones[:, :], 1.0), consts)
            pool.do(lambda e: e.memset(taken[:, :], 0.0), consts)
            pool.do(lambda e: e.iota(expert_no[:, :], pattern=[[1, E]], base=0, channel_multiplier=0,
                                     allow_small_or_imprecise_dtypes=True), consts)
            m = pool.do(lambda e: e.iota(blank[:, :, 0], pattern=[[0, E]], base=N, channel_multiplier=1), consts)
            mark["consts"] = m
            for q in (pool, dve, pe, act):
                q.wait(m)
            act.do(lambda e: e.activation(prob_sum[:, 0:TB], minus_half[:, :], ACT.Exp), act_fn)

        def small_inputs():
            load(in_const, mask_cols_in[:, :], mask_cols)
            load(in_const, bias_row[:, :], gate_bias.broadcast_to([P, E]))

        def scale_of_values():
            dve.wait((in_const, in_const.value))
            m = dve.do(lambda e: e.tensor_scalar(value_scale[:, :], mask_cols_in[:, :], V_S / (W_S * C_S), None, ALU.mult),
                       dve_route)
            act.wait(m)
            dve.wait(m)

        def blank_rows():
            load(out_blank, slot_table.rearrange("(p e) c -> p (e c)", e=E), blank[:, :, :].rearrange("p e c -> p (e c)"),
                 mark["consts"])
            load(out_blank, xn2_rows[N:N + CAP, :], xn2[:, 0, :])
            load(out_blank, out[N:N + CAP, :], xn2[:, 0, :])
            mark["blank"] = (out_blank, out_blank.value)

        weight_jobs = []

        def weight_job(name, dst, src, rows, cols):
            weight_jobs.append((name, dst, src, rows, cols))

        def rows_of(w):
            return w.rearrange("(k p) n -> p k n", p=P)

        def plan_weights():
            weight_job("wk", wk_s, rows_of(wk), KC, KV * HD)
            weight_job(("wq", 0), wq_s[:, :, 0:512], rows_of(wq)[:, :, 0:512], KD, 512)
            weight_job("wv", wv_s, rows_of(wv), KC, KV * HD)
            for c in range(4):
                if c:
                    weight_job(("wq", c), wq_s[:, :, c * 512:(c + 1) * 512], rows_of(wq)[:, :, c * 512:(c + 1) * 512], KD, 512)
                weight_job(("wo", c), wo_s[:, 4 * c:4 * c + 4, :], rows_of(wo)[:, 4 * c:4 * c + 4, :], 4, D)
            weight_job("gate", gate_s, rows_of(gate_t), KD, E)
            weight_job("sg", sg_s, rows_of(shared_gate), KD, FS)
            weight_job("su", su_s, rows_of(shared_up), KD, FS)
            weight_job("sd", sd_s, rows_of(shared_down), FSB, D)

        loaded, prepared = [0], [0]

        def load_weight():
            if loaded[0] == len(weight_jobs):
                return
            n = loaded[0]
            name, dst, src, rows, cols = weight_jobs[n]
            buf = weight_in[n % 2][:, 0:rows * cols].rearrange("p (k n) -> p k n", k=rows)
            mark["in", name] = load(in_weight[n % 2], buf, src, mark.get(("weight_free", n % 2)))
            loaded[0] += 1

        def prepare_weight():
            n = prepared[0]
            name, dst, src, rows, cols = weight_jobs[n]
            buf = weight_in[n % 2][:, 0:rows * cols].rearrange("p (k n) -> p k n", k=rows)
            prepared[0] += 1
            for k in range(rows):
                mark[name] = mark["weight_free", n % 2] = split_sbuf(buf[:, k], dst[:, k], W_S, mark["in", name], on_act=True)
                if k < rows - 1:
                    yield
            load_weight()
            yield

        def load_x(b):
            mark["x", b] = load(in_x[b % 2], x_in[b % 2][:, :, :],
                                x[b * T:(b + 1) * T, :].rearrange("(t p) d -> p t d", p=P), mark.get(("x1", b - 2)))

        def load_ctx(b):
            mark["ctx_in", b] = load(in_ctx, ctx_in[:, :, :], ctx_t[:, b * S:(b + 1) * S].rearrange("(k p) s -> p k s", p=P),
                                     mark.get(("ctx", b - 1)))

        def prepare_ctx(b):
            mark["ctx", b] = split_sbuf(ctx_in[:, :, :], ctx_s[b % 2], C_S, mark["ctx_in", b],
                                        mark.get(("key_pe", (b - 1) * KV - 1)))

        def load_mask(b):
            mark["mask_in", b] = load(in_mask, mask_in[:, :], mask[b:b + 1, :].broadcast_to([P, S]),
                                      mark.get(("mask", b - 1)))

        def prepare_mask(b):
            pool.wait(mark["mask_in", b], mark.get(("max", (b - 1) * KV - 1)))
            mark["mask", b] = pool.do(lambda e: e.tensor_scalar(mask_add[b % 2][:, :], mask_in[:, :], -1.0, MASKED,
                                                                ALU.add, ALU.mult), pool_mask)

        def layer_norm(src, dst, ready, free):
            dve.wait(ready, mark.get("rstd"))
            for t in range(TB):
                m = dve.do(lambda e, t=t: e.bn_stats(stats[:, t, :], src[:, t, :]), dve_stats)
                if t < TB - 1:
                    yield
            dve.wait(m)
            for t in range(TB):
                m = dve.do(lambda e, t=t: e.bn_aggr(mean_var[:, t, :], stats[:, t, :]), dve_stats)
            pool.wait(m, mark.get("normed_last"))
            m = pool.do(lambda e: e.tensor_scalar(var_eps[:, :], mean_var[:, :, 1], LN_EPS, 1.0, ALU.add, ALU.mult), pool_rstd)
            pool.wait(m)
            m = mark["rstd"] = pool.do(lambda e: e.tensor_tensor(rstd[:, :], var_eps[:, :], minus_half[:, :], ALU.pow), pool_rstd)
            yield
            yield
            dve.wait(m, *free)
            for t in range(TB):
                mark["normed_last"] = dve.do(lambda e, t=t: e.tensor_scalar(
                    dst[:, t, :], src[:, t, :], mean_var[:, t, 0:1], rstd[:, t:t + 1], ALU.subtract, ALU.mult), dve_normed)

        def transpose_rows(src, dst, t, ready, free, scale):
            fill, ps = filler_bank()
            pe.wait(ready, bank_free.get(fill))
            for k in range(KD):
                m = pe.do(lambda e, k=k: e.transpose(ps[:, k * P:(k + 1) * P], src[:, t, k * P:(k + 1) * P], ident[:, :]),
                          pe_fill if k == KD - 1 else None)
            act.wait(*free)
            r = split_psum(ps[:, :].rearrange("p (k t) -> p k t", k=KD), dst[:, :, t * P:(t + 1) * P], scale, m)
            bank_free[fill] = r
            return r

        def query(i, h):
            b, g = divmod(i, KV)
            pe.wait(mark["xn_t", b], mark["wq", g // 2], bank_free.get("query"))
            n = (g * PAIR + h) * HD
            m = products(ps_query[:, h * T:(h + 1) * T],
                         [(wq_s[:, k, n:n + HD], xn_t[b % 2][:, k, :]) for k in range(KD)],
                         pe_query if h == PAIR - 1 else None)
            if h < PAIR - 1:
                return
            act.wait(mark.get(("score_pe", i - 1)))
            mark["query_pe", i] = m
            mark["query", i] = bank_free["query"] = split_psum(ps_query[:, :], q_t, 1.0 / (W_S * X_S), m)

        def key(i):
            b, g = divmod(i, KV)
            pe.wait(mark["ctx", b], mark["wk"], bank_free.get("fill0"))
            m = products(ps_fill[0][:, 0:S], [(wk_s[:, k, g * HD:(g + 1) * HD], ctx_s[b % 2][:, k, :]) for k in range(KC)], pe_key)
            mark["key_pe", i] = m
            act.wait(mark.get(("score_pe", i - 1)))
            mark["key", i] = bank_free["fill0"] = split_psum(ps_fill[0][:, 0:S], k_t, 1.0 / (W_S * C_S), m)

        def value(b, half, s):
            cols = slice(half * 512, (half + 1) * 512)
            fill, ps = filler_bank()
            pe.wait(mark["ctx", b], mark["wv"], bank_free.get(fill))
            m = products(ps[:, :], [(ctx_s[b % 2][:, k, s * P:(s + 1) * P], wv_s[:, k, cols]) for k in range(KC)], pe_fill)
            act.wait(mark.get(("head_pe", (b - 1) * KV - 1)))
            n = b * SB + s
            mark["value", b, half, s] = bank_free[fill] = split_psum(
                ps[:, :], v_s[b % 2][:, s, cols], None, m, vector_scale=value_scale[:, n:n + 1])

        def scores(i):
            pe.wait(mark["query", i], mark["key", i], bank_free.get("score"))
            for h in range(PAIR):
                for t in range(TB):
                    c = h * T + t * P
                    m = products(ps_score[h][:, t * S:(t + 1) * S], [(q_t[:, c:c + P], k_t)],
                                 pe_score if t == TB - 1 else None)
                mark["score_pe", i, h] = m
            mark["score_pe", i] = m

        def softmax_exp(i):
            b = i // KV
            dve.wait(mark["mask", b], mark.get(("low", i - 1)), mark.get(("norm", i - 1)))
            for c in range(PAIR * TB):
                h, t = divmod(c, TB)
                dve.wait(mark["score_pe", i, h])
                m = dve.do(lambda e, c=c, h=h, t=t: e.tensor_tensor_reduce(
                    out=probs[:, c, :], in0=ps_score[h][:, t * S:(t + 1) * S], in1=mask_add[b % 2][:, :],
                    scale=-SCORE_SCALE, scalar=3e38, op0=ALU.add, op1=ALU.min, accum_out=neg_max[:, c:c + 1]), dve_max)
                act.wait(m)
                a = act.do(lambda e, c=c: e.activation(probs[:, c, :], probs[:, c, :], ACT.Exp, bias=neg_max[:, c:c + 1],
                                                       scale=-1.0, accum_out=prob_sum[:, c:c + 1]), act_exp)
            mark["max", i] = bank_free["score"] = m
            mark["exp", i] = a

        def softmax_norm(i):
            dve.wait(mark["exp", i], mark.get(("norm", i - 1)))
            r = dve.do(lambda e: e.reciprocal(prob_inv[:, :], prob_sum[:, :]), dve_inv)
            dve.wait(r)
            r = dve.do(lambda e: e.tensor_scalar(prob_scale[:, :], prob_inv[:, :], P_S, None, ALU.mult), dve_inv)
            pool.wait(r, mark.get(("probs", i - 1)))
            for c in range(PAIR * TB):
                mark["norm", i, c] = pool.do(lambda e, c=c: e.tensor_scalar(
                    p_rows[:, 0, c, :], probs[:, c, :], prob_scale[:, c:c + 1], 1.0, ALU.mult, ALU.mult), pool_norm)
            mark["norm", i] = mark["norm", i, PAIR * TB - 1]
            dve.wait(r)

        def softmax_low(i, cs):
            for c in cs:
                dve.wait(mark["norm", i, c])
                mark["low", i] = dve.do(lambda e, c=c: e.scalar_tensor_tensor(
                    p_rows[:, 1, c, :], probs[:, c, :], prob_scale[:, c:c + 1], p_rows[:, 0, c, :], ALU.mult, ALU.subtract),
                    dve_low)

        def transpose_probs(i):
            sync.wait(mark["norm", i], mark["low", i], mark.get(("head_pe", i - 1)), mark.get(("probs", i - 1)))
            mark["probs", i] = sync.do(lambda e: e.dma_start_transpose(
                p_both[:, :, :, :, :].rearrange("p h c s t -> p (h c s) t"),
                p_rows[:, :, :, :].rearrange("p h c s -> p (h c s)")), turned, 16)

        def attend(i):
            b, g = divmod(i, KV)
            pe.wait(mark["probs", i], mark["value", b, g // 4, 0], mark["value", b, g // 4, 1], bank_free.get("head"))
            m = products(ps_head[:, :], [(v_s[b % 2][:, s, g * HD:(g + 1) * HD], p_t[s]) for s in range(SB)], pe_head)
            mark["head_pe", i] = m
            act.wait(mark.get(("out_pe", i - 1)))
            mark["head", i] = bank_free["head"] = split_psum(ps_head[:, :], o_t, 1.0 / P_S, m)

        def project(i):
            b, g = divmod(i, KV)
            pe.wait(mark["head", i], mark["wo", g // 2], bank_free.get("out") if g == 0 else None)
            for t in range(TB):
                m = products(ps_out[t][:, :], [(o_t[:, h * T + t * P:h * T + (t + 1) * P], wo_s[:, g * PAIR + h, :])
                                               for h in range(PAIR)],
                             pe_out if t == TB - 1 else None, first=g == 0, last=g == KV - 1)
            mark["out_pe", i] = m

        def residual(b):
            dve.wait(mark["out_pe", b * KV + KV - 1], mark["x", b], mark.get(("rows_out", b - 1)))
            for t in range(TB):
                m = dve.do(lambda e, t=t: e.scalar_tensor_tensor(x1[:, t, :], ps_out[t][:, :], 1.0 / (V_S * W_S),
                                                                 x_in[b % 2][:, t, :], ALU.mult, ALU.add), dve_residual)
                mark["x1", b] = bank_free["out"] = m
                yield

        def gate(b):
            fill, ps = filler_bank()
            pe.wait(mark["xn2_t", b], mark["gate"], bank_free.get(fill))
            for t in range(TB):
                m = products(ps[:, t * E:(t + 1) * E],
                             [(xn2_t[:, k, t * P:(t + 1) * P], gate_s[:, k, :]) for k in range(KD)],
                             pe_fill if t == TB - 1 else None)
            act.wait(m)
            m = act.do(lambda e: e.activation(exp_neg[:, :, :], ps[:, 0:TB * E].rearrange("p (t e) -> p t e", e=E),
                                              ACT.Exp, scale=-1.0 / (W_S * X_S)), act_fn)
            bank_free[fill] = mark["exp_neg", b] = m

        def chain(build_):
            m = dve.do(build_, dve_route)
            dve.wait(m)
            return m

        def choose(b):
            dve.wait(mark["exp_neg", b])
            chain(lambda e: e.tensor_scalar(exp_neg[:, :, :], exp_neg[:, :, :], 1.0, None, ALU.add))
            chain(lambda e: e.reciprocal(score[:, :, :], exp_neg[:, :, :]))
            mark["score_read", b] = chain(lambda e: e.tensor_tensor(
                biased[:, :, :], score[:, :, :], bias_row[:, :].unsqueeze(1).broadcast_to([P, TB, E]), ALU.add))
            yield
            flat = biased[:, :, :].rearrange("p t e -> p (t e)")
            for g in range(TB * GROUPS):
                m = dve.do(lambda e, g=g: e.max(group_top[:, g, :], flat[:, g * EPG:(g + 1) * EPG]), dve_route)
            dve.wait(m)
            yield
            top = group_top[:, :, :].rearrange("p (t g) k -> p t g k", t=TB)
            chain(lambda e: e.tensor_tensor(group_score[:, :, :], top[:, :, :, 0], top[:, :, :, 1], ALU.add))
            yield
            full = [P, TB, GROUPS, GROUPS]
            mine = group_score[:, :, :].unsqueeze(3).broadcast_to(full)
            other = group_score[:, :, :].unsqueeze(2).broadcast_to(full)
            dve.do(lambda e: e.tensor_tensor(beats[:, :, :, :], other, mine, ALU.is_gt))
            chain(lambda e: e.tensor_tensor(ties[:, :, :, :], other, mine, ALU.is_equal))
            chain(lambda e: e.tensor_tensor(ties[:, :, :, :], ties[:, :, :, :],
                                            lower[:, :, :].unsqueeze(1).broadcast_to(full), ALU.mult))
            chain(lambda e: e.tensor_tensor(beats[:, :, :, :], beats[:, :, :, :], ties[:, :, :, :], ALU.add))
            yield
            chain(lambda e: e.reduce_sum(group_rank[:, :, :], beats[:, :, :, :], AX.X))
            chain(lambda e: e.tensor_scalar(group_rank[:, :, :], group_rank[:, :, :], float(TOPG), None, ALU.is_lt))
            yield
            by_group = biased[:, :, :].rearrange("p t (g e) -> p (t g) e", g=GROUPS)
            chain(lambda e: e.tensor_tensor(by_group, by_group, group_rank[:, :, :].rearrange("p t g -> p (t g)")
                                            .unsqueeze(2).broadcast_to([P, TB * GROUPS, EPG]), ALU.mult))
            for t in range(TB):
                m = dve.do(lambda e, t=t: e.max(top8[:, t, :], biased[:, t, :]), dve_route)
            dve.wait(m)
            yield
            for t in range(TB):
                m = dve.do(lambda e, t=t: e.max_index(top8_at[:, t, :], top8[:, t, :], biased[:, t, :]), dve_route)
            dve.wait(m)
            yield
            chain(lambda e: e.tensor_copy(chosen[:, :, :], top8_at[:, :, 0:TOPK]))
            for t in range(TB):
                m = dve.do(lambda e, t=t: e.tensor_tensor(
                    one_hot[:, t, :, :], expert_no[:, :].unsqueeze(1).broadcast_to([P, TOPK, E]),
                    chosen[:, t, :].unsqueeze(2).broadcast_to([P, TOPK, E]), ALU.is_equal), dve_route)
            yield
            dve.wait(m, mark.get(("rank_pe", b - 1)))

            def count_uses(e):
                with nc.allow_low_precision(reason="0 and 1 are exact in float16"):
                    return e.reduce_sum(uses[:, :, :], one_hot[:, :, :, :].rearrange("p t k e -> p t e k"), AX.X)
            mark["uses", b] = dve.do(count_uses, dve_route)
            yield
            yield from pick(score, weight)
            yield
            chain(lambda e: e.reduce_sum(weight_sum[:, :], weight[:, :, :], AX.X))
            chain(lambda e: e.tensor_scalar(weight_sum[:, :], weight_sum[:, :], 1e-20, None, ALU.add))
            chain(lambda e: e.reciprocal(weight_inv[:, :], weight_sum[:, :]))
            chain(lambda e: e.tensor_scalar(weight_inv[:, :], weight_inv[:, :], ROUTE_SCALE, None, ALU.mult))
            yield
            dve.wait(mark.get(("scattered", b - 2)))
            mark["weight", b] = dve.do(lambda e: e.tensor_tensor(
                entry[b % 2][:, :, :, 1].bitcast(F32), weight[:, :, :], weight_inv[:, :].unsqueeze(2).broadcast_to([P, TB, TOPK]),
                ALU.mult), dve_route)
            yield

        def pick(table_, dst):
            for t in range(TB):
                m = dve.do(lambda e, t=t: e.tensor_tensor(
                    picked[:, t, :, :], one_hot[:, t, :, :], table_[:, t, :].unsqueeze(1).broadcast_to([P, TOPK, E]), ALU.mult),
                    dve_route)
            dve.wait(m)
            yield
            chain(lambda e: e.reduce_sum(dst[:, :, :], picked[:, :, :, :], AX.X))

        def rank(b):
            fill, ps = filler_bank()
            pe.wait(mark["uses", b], bank_free.get(fill))
            for t in range(TB):
                for u in range(t + 1):
                    pe.do(lambda e, t=t, u=u: e.matmul(ps[:, t * E:(t + 1) * E], (earlier if u == t else ones)[:, :],
                                                       uses[:, u, :], start=u == 0, stop=u == t))
            for u in range(TB):
                m = pe.do(lambda e, u=u: e.matmul(ps[:, TB * E:(TB + 1) * E], ones[:, :], uses[:, u, :], start=u == 0,
                                                  stop=u == TB - 1), pe_fill if u == TB - 1 else None)
            mark["rank_pe", b] = m

        def place(b):
            fill, ps = filler_bank()
            dve.wait(mark["rank_pe", b])
            chain(lambda e: e.tensor_tensor(position[:, :, :], ps[:, 0:TB * E].rearrange("p (t e) -> p t e", e=E),
                                            taken[:, :].unsqueeze(1).broadcast_to([P, TB, E]), ALU.add))
            bank_free[fill] = chain(lambda e: e.tensor_tensor(taken[:, :], ps[:, TB * E:(TB + 1) * E], taken[:, :], ALU.add))

        def find_slots(b):
            yield from pick(position, my_position)
            chain(lambda e: e.scalar_tensor_tensor(slot_f[:, :, :], my_position[:, :, :], float(E), chosen[:, :, :],
                                                   ALU.mult, ALU.add))
            mark["slot", b] = dve.do(lambda e: e.tensor_copy(slot_at[b % 2][:, :, :], slot_f[:, :, :]), dve_route)
            yield

        def record(b, tiles):
            if 0 in tiles:
                pool.wait(mark.get(("scattered", b - 2)))
                m = pool.do(lambda e: e.iota(entry[b % 2][:, :, :, 0], pattern=[[P, TB], [0, TOPK]], base=b * T,
                                             channel_multiplier=1), pool_entry)
                pool.wait(m, mark["weight", b], mark["slot", b], mark["blank"])
            for t in tiles:
                for k in range(TOPK):
                    m = pool.do(lambda e, t=t, k=k: e.indirect_dma_start(
                        slot_table, bass.IndirectOffsetOnAxis(ap=slot_at[b % 2][:, t, k:k + 1], axis=0),
                        entry[b % 2][:, t, k, :], None, bounds_check=CAP * E - 1, oob_is_err=False), scattered[b % 2], 16)
            mark["scattered", b] = m

        def swiglu(g_psum, u_psum, dst, scale, ready, free):
            k = 1.0 / (W_S * X_S)
            act.wait(ready, mark.get("glu_last"))
            m = act.do(lambda e: e.activation(tanh_g[:, :], g_psum, ACT.Tanh, scale=0.5 * k), act_fn)
            dve.wait(m)
            m = dve.do(lambda e: e.scalar_tensor_tensor(gated[:, :], tanh_g[:, :], 1.0, g_psum, ALU.add, ALU.mult), dve_glu)
            dve.wait(m, *free)
            m = dve.do(lambda e: e.scalar_tensor_tensor(dst, gated[:, :], 0.5 * k * k * scale, u_psum, ALU.mult, ALU.mult), dve_glu)
            mark["glu_last"] = m
            return m

        def shared_up_part(b, f):
            shared_up_products(b, f)
            shared_up_glu(b, f)

        def shared_up_products(b, f):
            fill, ps = filler_bank()
            pe.wait(mark["xn2_t", b], mark["sg"], mark["su"], bank_free.get(fill))
            for n, w in enumerate((sg_s, su_s)):
                m = products(ps[:, n * T:(n + 1) * T], [(w[:, k, f * P:(f + 1) * P], xn2_t[:, k, :]) for k in range(KD)],
                             pe_fill if n else None)
            mark["xn2_t_read", b] = mark["shared_up", b, f] = m

        def shared_up_glu(b, f):
            fill, ps = filler_bank()
            m = bank_free[fill] = swiglu(ps[:, 0:T], ps[:, T:2 * T], hidden[:, :], HS_S, mark["shared_up", b, f],
                                         [mark.get("hidden_read")])
            if b == B - 1:
                mark["hidden", b] = mark["hidden_read"] = split_sbuf(hidden[:, :], h_t[:, f, :], 1.0, m,
                                                                     mark.get(("shared_pe", b - 1)), on_act=True)
                return
            pool.wait(m, mark.get(("shared_pe", b - 1)))
            m = pool.do(lambda e: e.tensor_scalar(h_t.hi[:, f, :], hidden[:, :], 1.0, 1.0, ALU.mult, ALU.mult), pool_hi)
            pool.wait(m)
            mark["hidden", b] = mark["hidden_read"] = pool.do(
                lambda e: e.tensor_tensor(h_t.lo[:, f, :], hidden[:, :], h_t.hi[:, f, :], ALU.subtract), pool_hi)

        def shared_down_part(b, t):
            fill, ps = filler_bank()
            pe.wait(mark["hidden", b], mark["sd"], bank_free.get(fill))
            m = products(ps[:, :], [(h_t[:, f, t * P:(t + 1) * P], sd_s[:, f, :]) for f in range(FSB)], pe_fill)
            mark["shared_pe", b] = m
            dve.wait(m, mark["x1", b])
            m = bank_free[fill] = dve.do(lambda e: e.scalar_tensor_tensor(
                x1[:, t, :], ps[:, :], 1.0 / (HS_S * W_S), x1[:, t, :], ALU.mult, ALU.add), dve_residual)
            r = b * T + t * P
            mark["rows_out", b] = load(out_rows, out[r:r + P, :], x1[:, t, :], m)

        def normalise_x(b):
            yield from layer_norm(x_in[b % 2], normed, mark["x", b], [mark.get(("xn_t", b - 1))])
            mark["normed", b] = mark["normed_last"]
            yield

        def x_t(b, t):
            mark["xn_t", b] = transpose_rows(normed, xn_t[b % 2], t, mark["normed", b],
                                             [mark.get(("query_pe", (b - 1) * KV - 1))], X_S)

        def normalise_x1(b):
            yield from layer_norm(x1, xn2, mark["x1", b],
                                  [mark.get(("xn2_out", b - 1)), mark.get(("xn2_t", b - 1)), mark["blank"]])
            m = mark["xn2", b] = mark["normed_last"]
            mark["xn2_out", b] = load(out_xn2, xn2_rows[b * T:(b + 1) * T, :].rearrange("(t p) d -> p t d", p=P),
                                      xn2[:, :, :], m)
            yield

        def xn2_transposed(b, t):
            mark["xn2_t", b] = transpose_rows(xn2, xn2_t, t, mark["xn2", b], [mark.get(("xn2_t_read", b - 1))], X_S)

        def fillers(b, j):
            ahead, behind = b + 1 < B, 0 <= b - 1
            a, z = b + 1, b - 1
            none = lambda: None
            if b == 0 and j < 6:
                tiles = [(b_, half, s_) for b_ in (0, 1) for half in range(2) for s_ in range(SB)][SB:]
                return (lambda: x_t(1, j - 4)) if j in (4, 5) else none, (lambda: value(*tiles[j]))
            table_ = {
                0: [ahead and (lambda: value(a, 0, 0)), ahead and (lambda: value(a, 0, 1))],
                1: [ahead and (lambda: value(a, 1, 0)), ahead and (lambda: value(a, 1, 1))],
                2: [behind and (lambda: xn2_transposed(z, 0)), behind and (lambda: xn2_transposed(z, 1))],
                3: [behind and (lambda: gate(z)), behind and (lambda: shared_up_part(z, 0))],
                4: [ahead and (lambda: x_t(a, 0)), behind and (lambda: shared_up_part(z, 1))],
                5: [ahead and (lambda: x_t(a, 1)), behind and (lambda: shared_up_part(z, 2))],
                6: [behind and (lambda: (rank(z), place(z))), behind and (lambda: shared_up_part(z, 3))],
                7: [behind and (lambda: shared_down_part(z, 0)), behind and (lambda: shared_down_part(z, 1))],
            }
            return [f or none for f in table_[j]]

        def begin_side_work(b, j):
            ahead, behind = b + 1 < B, 0 <= b - 1
            if j == 1:
                finish("residual")
                if behind:
                    begin("x1 normed", normalise_x1(b - 1))
                if ahead:
                    load_x(b + 1)
                    load_mask(b + 1)
            if j == 2 and ahead:
                prepare_mask(b + 1)
            if j == 4 and b + 2 < B:
                load_ctx(b + 2)

        before_fillers = {2: "x1 normed", 4: "x normed", 6: "chosen"}

        def prologue():
            plan_weights()
            load_x(0)
            load_ctx(0)
            load_weight()
            load_weight()
            load_mask(0)
            small_inputs()
            constants()
            begin("x", normalise_x(0))
            finish("x")
            for t in range(TB):
                use[0] = t
                x_t(0, t)
            prepare_ctx(0)
            for name in ("wk", "wq"):
                begin(name, prepare_weight())
                finish(name)
            key(0)
            scale_of_values()
            begin("wv", prepare_weight())
            finish("wv")
            for h in range(PAIR):
                query(0, h)
            prepare_mask(0)
            blank_rows()
            load_ctx(1)

        prepare_at = {0: 2, 1: 1, 2: 1, 3: 1, 4: 1, 5: 1, 6: 1, 7: 1, 8: 1, 10: 1}

        def attention():
            for i in range(TURNS + 1):
                b, j = divmod(i, KV)
                for _ in range(prepare_at.get(i, 0)):
                    begin("weight", prepare_weight())
                if i < TURNS:
                    begin_side_work(b, j)
                    scores(i)
                    softmax_exp(i)
                if i == 0:
                    for s in range(SB):
                        use[0] = 1 - s
                        value(0, 0, s)
                    prepare_ctx(1)
                if i + 1 < TURNS:
                    key(i + 1)
                    query(i + 1, 0)
                piece()
                if i < TURNS:
                    softmax_norm(i)
                if j in before_fillers:
                    finish(before_fillers[j])
                first, second = fillers(b, j) if i < TURNS else (lambda: None,) * 2
                use[0] = 1
                first()
                if i < TURNS and b and j == 3:
                    begin("chosen", choose(b - 1))
                if i < TURNS and b and j == 6:
                    begin("slots", find_slots(b - 1))
                piece()
                if i < TURNS:
                    softmax_low(i, range(0, PAIR * TB // 2))
                if i:
                    attend(i - 1)
                if i < TURNS:
                    softmax_low(i, range(PAIR * TB // 2, PAIR * TB))
                    transpose_probs(i)
                if j == 2 and b + 1 < B:
                    begin("x normed", normalise_x(b + 1))
                piece()
                if i + 1 < TURNS:
                    query(i + 1, 1)
                piece()
                use[0] = 0
                second()
                piece()
                if i:
                    project(i - 1)
                piece()
                if prepare_at.get(i, 0):
                    finish("weight")
                if i < TURNS and j == 7:
                    if b + 2 < B:
                        prepare_ctx(b + 2)
                    if b:
                        finish("slots")
                        record(b - 1, [0])
                if i and j == 0:
                    if b > 1:
                        record(b - 2, [1])
                    begin("residual", residual(b - 1))
                piece()

        def expert_views(n):
            w = expert_in[n % AHEAD]
            up = w[:, 0:KD * 2 * F].rearrange("p (k n) -> p k n", k=KD)
            down = w[:, KD * 2 * F:].rearrange("p (k n) -> p k n", k=FB)
            return up, down

        def load_expert(e_):
            up, down = expert_views(e_)
            over_wo = (e_ + 1) * 2 * EW > sum(2 * k * n for k, n in sizes[:3])
            after = [mark.get(("expert_split", e_ - AHEAD)), mark["query_pe", TURNS - 1], mark["key_pe", TURNS - 1],
                     mark["out_pe", TURNS - 1] if over_wo else None]
            sig = in_expert[e_ % AHEAD]
            load(sig, up[:, :, 0:F], w1[e_].rearrange("(p k) n -> p k n", p=P), *after)
            load(sig, up[:, :, F:2 * F], w3[e_].rearrange("(p k) n -> p k n", p=P))
            mark["expert_in", e_] = load(sig, down, w2[e_].rearrange("(p k) n -> p k n", p=P))

        def expert_high(e_, part):
            src, dst = expert_in[e_ % AHEAD], expert_w[e_ % HELD]
            third = EW // 3
            at = slice(part * third, (part + 1) * third)
            free = [mark.get(("expert_up_pe" if part < 2 else "expert_y_pe", e_ - HELD)), mark["out_pe", TURNS - 1]]
            if part < 2:
                act.wait(mark["expert_in", e_], *free)
                m = act.do(lambda e: e.activation(dst.hi[:, at], src[:, at], ACT.Copy, scale=W_S), act_hi)
            else:
                pool.wait(mark["expert_in", e_], *free)
                m = pool.do(lambda e: e.tensor_scalar(dst.hi[:, at], src[:, at], W_S, 1.0, ALU.mult, ALU.mult), pool_hi)
            mark["expert_high", e_, part] = m

        def expert_low(e_, part):
            src, dst = expert_in[e_ % AHEAD], expert_w[e_ % HELD]
            third = EW // 3
            at = slice(part * third, (part + 1) * third)
            dve.wait(mark["expert_in", e_], mark["expert_high", e_, part])
            mark["expert_split", e_] = dve.do(lambda e: e.scalar_tensor_tensor(
                dst.lo[:, at], src[:, at], W_S, dst.hi[:, at], ALU.mult, ALU.subtract), dve_lo)

        def load_table():
            m = load(in_table, table[:, :, :].rearrange("p e c -> p (e c)"), slot_table.rearrange("(p e) c -> p (e c)", e=E),
                     mark["scattered", B - 1], mark["scattered", B - 2])
            dve.wait(m)
            pool.wait(m)
            mark["slot_weight"] = dve.do(lambda e: e.tensor_scalar(slot_weight[:, :], table[:, :, 1].bitcast(F32),
                                                                   1.0 / (HE_S * W_S), None, ALU.mult), dve_route)
            act.wait(mark["slot_weight"])

        def gather(e_):
            pool.wait(mark.get(("rows_pe", e_ - 3)), mark["xn2_out", B - 1], mark["x1", B - 1], mark["x1", B - 2])
            mark["gathered", e_] = pool.do(lambda e: e.indirect_dma_start(
                rows_in[e_ % 3], None, xn2_rows, bass.IndirectOffsetOnAxis(ap=table[:, e_, 0:1], axis=0),
                bounds_check=N + CAP - 1, oob_is_err=True), gathered[e_ % 3], 16)

        def expert_rows(e_):
            rows = rows_in[e_ % 3].rearrange("c (p k) -> c k p", k=KD)
            ps = ps_fill[e_ % 2]
            pe.wait(mark["gathered", e_], bank_free.get(f"fill{e_ % 2}"))
            for k in range(KD):
                m = pe.do(lambda e, k=k: e.transpose(ps[:, k * P:(k + 1) * P], rows[:, k, :], ident[:, :]),
                          pe_fill if k == KD - 1 else None)
            mark["rows_pe", e_] = m
            act.wait(mark.get(("expert_up_pe", e_ - 2)), mark["query_pe", TURNS - 1])
            mark["rows_t", e_] = bank_free[f"fill{e_ % 2}"] = split_psum(
                ps[:, :].rearrange("p (k c) -> p k c", k=KD), rows_t[e_ % 2][:, :, 0:P], X_S, m)

        def expert_up(e_):
            ps = ps_score[e_ % 2]
            w = expert_w[e_ % HELD][:, 0:KD * 2 * F]
            pe.wait(mark["rows_t", e_], mark["expert_split", e_], bank_free.get(f"up{e_ % 2}", bank_free[f"fill{2 + e_ % 2}"]))
            m = products(ps[:, :], [(rows_t[e_ % 2][:, k, 0:P], w[:, k * 2 * F:(k + 1) * 2 * F]) for k in range(KD)], pe_score)
            mark["expert_up_pe", e_] = m
            mark["expert_h", e_] = bank_free[f"up{e_ % 2}"] = swiglu(
                ps[:, 0:F], ps[:, F:2 * F], expert_h, HE_S, m, [mark.get(("expert_ht_pe", e_ - 1)), mark["xn_t", B - 1]])

        def expert_hidden(e_):
            cols = expert_h.rearrange("c (p f) -> c f p", f=FB)
            ps = (ps_head, ps_query)[e_ % 2]
            pe.wait(mark["expert_h", e_], bank_free.get(("head", "query")[e_ % 2]))
            for f in range(FB):
                m = pe.do(lambda e, f=f: e.transpose(ps[:, f * P:(f + 1) * P], cols[:, f, :], ident[:, :]),
                          pe_trans if f == FB - 1 else None)
            mark["expert_ht_pe", e_] = m
            act.wait(mark.get(("expert_y_pe", e_ - 2)), mark[("shared_pe", B - 1)])
            mark["expert_ht", e_] = bank_free[("head", "query")[e_ % 2]] = split_psum(
                ps[:, 0:FB * P].rearrange("p (f c) -> p f c", f=FB), expert_h_t[e_ % 2], 1.0, m)

        def expert_down(e_):
            ps = ps_out[e_ % 2]
            w = expert_w[e_ % HELD][:, KD * 2 * F:]
            pe.wait(mark["expert_ht", e_], bank_free.get(f"y{e_ % 2}"), bank_free.get("out"))
            m = products(ps[:, :], [(expert_h_t[e_ % 2][:, f, :], w[:, f * D:(f + 1) * D]) for f in range(FB)], pe_out)
            mark["expert_y_pe", e_] = m
            if e_ + HELD < E:
                expert_high(e_ + HELD, 2)
            act.wait(m, mark.get(("added", e_ - 4)), mark["sd"])
            m = bank_free[f"y{e_ % 2}"] = act.do(lambda e: e.activation(
                expert_y[e_ % 4], ps[:, :], ACT.Copy, scale=slot_weight[:, e_:e_ + 1]), act_y)
            pool.wait(m, mark.get(("added", e_ - 1)), mark["rows_out", B - 1])
            mark["added", e_] = pool.do(lambda e: e.indirect_dma_start(
                out, bass.IndirectOffsetOnAxis(ap=table[:, e_, 0:1], axis=0), expert_y[e_ % 4], None,
                bounds_check=N + CAP - 1, oob_is_err=True, compute_op=ALU.add), added, 16)

        def tail():
            z = B - 1
            for e_ in range(AHEAD):
                load_expert(e_)
            finish("residual")
            begin("x1 normed", normalise_x1(z))
            piece()
            piece()
            for part in range(3):
                expert_high(0, part)
            expert_low(0, 0)
            finish("x1 normed")
            for e_ in range(1, HELD):
                expert_high(e_, 2)
            for t in range(TB):
                use[0] = 1 - t
                xn2_transposed(z, t)
            expert_low(0, 1)
            use[0] = 1
            gate(z)
            bank_free["fill2"] = bank_free["fill3"] = bank_free["score"]
            up_banks = [0, 2, 3, 1]
            for f in range(2):
                use[0] = up_banks[f]
                shared_up_products(z, f)
            expert_low(0, 2)
            for e_ in range(1, HELD):
                for part in range(2):
                    expert_high(e_, part)
            begin("chosen", choose(z))
            finish("chosen")
            use[0] = 1
            rank(z)
            expert_low(1, 0)
            place(z)
            begin("slots", find_slots(z))
            finish("slots")
            record(z, range(TB))
            for f in range(2, FSB):
                use[0] = up_banks[f]
                shared_up_products(z, f)
            for part in (1, 2):
                expert_low(1, part)
            load_expert(AHEAD)
            for f in range(FSB):
                use[0] = up_banks[f]
                shared_up_glu(z, f)
            for part in range(3):
                expert_low(2, part)
            load_table()
            for e_ in range(3):
                gather(e_)
            for t in range(TB):
                use[0] = t
                shared_down_part(z, t)
            for e_ in range(1, HELD):
                load_expert(AHEAD + e_)
            for e_ in range(2):
                expert_rows(e_)
                gather(e_ + 3)

        def experts():
            for e_ in range(E + 1):
                if e_ < E:
                    expert_up(e_)
                if e_ + HELD < E:
                    expert_high(e_ + HELD, 0)
                if e_ >= 1:
                    expert_down(e_ - 1)
                    if e_ - 1 + HELD < E:
                        expert_low(e_ - 1 + HELD, 1)
                if e_ < E:
                    expert_hidden(e_)
                if e_ + HELD < E:
                    expert_high(e_ + HELD, 1)
                    expert_low(e_ + HELD, 0)
                if 1 <= e_ <= E - HELD:
                    expert_low(e_ - 1 + HELD, 2)
                    if e_ - 1 + HELD + AHEAD < E:
                        load_expert(e_ - 1 + HELD + AHEAD)
                if e_ + 2 < E:
                    expert_rows(e_ + 2)
                if e_ + 5 < E:
                    gather(e_ + 5)
            pool.wait(mark["added", E - 1])
            sync.wait(mark["rows_out", B - 1], mark["xn2_out", B - 1], mark["blank"])

        prologue()
        attention()
        tail()
        experts()

        block = stack.enter_context(nc.Block())
        block.sync(sync.run)
        block.gpsimd(pool.run)
        block.scalar(act.run)
        block.vector(dve.run)
        block.tensor(pe.run)


def kernel(x, ctx_1024, mask_BxS2_bf1, L0_xattn_Wq, L0_xattn_Wk, L0_xattn_Wv, L0_xattn_Wo, L0_ffn_gate_w, L0_ffn_gate_bias,
           L0_ffn_w1, L0_ffn_w2, L0_ffn_w3, L0_ffn_shared_gate, L0_ffn_shared_up, L0_ffn_shared_down):
    import concourse.bacc as bacc
    from concourse.bass_utils import run_bass_kernel_spmd

    mask = np.ascontiguousarray(mask_BxS2_bf1).view(np.uint8)
    arrays = {
        "x": np.asarray(x).reshape(N, D),
        "ctx_t": np.asarray(ctx_1024).reshape(B * S, DC).T,
        "mask": mask,
        "mask_cols": mask.reshape(B * SB, P).T,
        "wq": L0_xattn_Wq, "wk": L0_xattn_Wk, "wv": L0_xattn_Wv, "wo": L0_xattn_Wo,
        "gate_t": np.asarray(L0_ffn_gate_w).T,
        "gate_bias": np.asarray(L0_ffn_gate_bias).reshape(1, E),
        "w1": L0_ffn_w1, "w2": L0_ffn_w2, "w3": L0_ffn_w3,
        "shared_gate": L0_ffn_shared_gate, "shared_up": L0_ffn_shared_up, "shared_down": L0_ffn_shared_down,
    }
    arrays = {k: np.ascontiguousarray(a) for k, a in arrays.items()}
    nc = bacc.Bacc("TRN2", target_bir_lowering=False, num_devices=1)
    args = [nc.dram_tensor(k, a.shape, mybir.dt.from_np(a.dtype), kind="ExternalInput").ap() for k, a in arrays.items()]
    out = nc.dram_tensor("out_rows_dram", (N + CAP, D), F32, kind="ExternalOutput").ap()
    build(nc, *args, out)
    got = run_bass_kernel_spmd(nc, [arrays], core_ids=[0])
    return got.results[0]["out_rows_dram"][:N].reshape(B, T, D)
```
